# Optimizing a Trainium2 kernel written in Bass

```python
import numpy as np
import jax
import jax.numpy as jnp

def _softmax(x, axis=-1):
    return jax.nn.softmax(x, axis=axis)

def _gelu(x):
    return jax.nn.gelu(x, approximate=True)

def _silu(x):
    return jax.nn.silu(x)

def _sigmoid(x):
    return jax.nn.sigmoid(x)

def _layernorm(x, axis=-1, eps=1e-05):
    m = jnp.mean(x, axis=axis, keepdims=True)
    v = jnp.var(x, axis=axis, keepdims=True)
    return (x - m) / jnp.sqrt(v + eps)

def _scatter_add(tgt, idx, src, axis=0):
    return tgt.at[idx].add(src)

def _segment_sum(src, seg, n):
    return jax.ops.segment_sum(src, seg, n)
kernel_name = 'mk_adj_preln_d4_adj_r2_f86ce2'

def setup_inputs(seed: int=0):
    np.random.seed(seed)
    _w = jnp.asarray

    def _rec_inputs():
        import jax
        import jax.numpy as jnp
        _gk = jax.random.key(seed)
        x = 7.22e-05 + 1 * jax.random.normal(jax.random.fold_in(_gk, 1), (64, 128, 256), jnp.float32)
        _a = jax.random.bernoulli(jax.random.fold_in(_gk, 2), 0.125, (64, 128, 128))
        _a = jnp.logical_or(_a, jnp.swapaxes(_a, -1, -2))
        _a = jnp.logical_or(_a, jnp.eye(128, dtype=bool))
        _af = _a.astype(jnp.float32)
        _af = _af * jax.random.uniform(jax.random.fold_in(_gk, 3), (64, 128, 128), jnp.float32, 0.05, 1)
        adj = _af
        _nm = jnp.ones((64, 128), dtype=bool)
        nodemask = jnp.where(_nm, 1.0, 0.0).astype(jnp.float32)
        return (x, adj, nodemask)
    x, adj, nodemask = _rec_inputs()

    def _L0_gnn_setup():
        import jax, jax.numpy as jnp
        import numpy as np
        B, N, IN_DIM, ATT_DIM = (2, 4096, 256, 256)
        key = jax.random.key(seed)
        k1, k2, k3, k4 = jax.random.split(key, 4)
        X = jax.random.normal(k1, (B, N, IN_DIM), dtype=jnp.float32)
        adj = jax.random.uniform(k2, (B, N, N), dtype=jnp.float32)
        mask = jnp.ones((B, N), dtype=jnp.float32)
        Wqk = jax.random.normal(k3, (IN_DIM, 2 * ATT_DIM), dtype=jnp.float32) / np.sqrt(IN_DIM)
        Wv = jax.random.normal(k4, (IN_DIM, IN_DIM), dtype=jnp.float32) / np.sqrt(IN_DIM)
        return {'X': X, 'adj': adj, 'mask': mask, 'Wqk': Wqk, 'Wv': Wv}
    _L0_gnn_all = _L0_gnn_setup()
    _L0_gnn_in = {k: v for k, v in _L0_gnn_all.items() if k in ('Wqk', 'Wv')}
    del _L0_gnn_all

    def _L1_gnn_setup():
        import jax, jax.numpy as jnp
        import numpy as np
        B, N, D = (8, 1024, 256)
        key = jax.random.key(seed)
        ks = jax.random.split(key, 8)
        scale = 0.5 / np.sqrt(D)
        x = jax.random.normal(ks[0], (B, N, D), dtype=jnp.float32)
        adj = jax.random.uniform(ks[1], (B, N, N), dtype=jnp.float32)
        Wq_w = jax.random.normal(ks[2], (D, D), dtype=jnp.float32) * scale
        Wk_w = jax.random.normal(ks[3], (D, D), dtype=jnp.float32) * scale
        Wv_w = jax.random.normal(ks[4], (D, D), dtype=jnp.float32) * scale
        Wq_b = jnp.zeros((D,), dtype=jnp.float32)
        Wk_b = jnp.zeros((D,), dtype=jnp.float32)
        Wv_b = jnp.zeros((D,), dtype=jnp.float32)
        return {'x': x, 'adj': adj, 'Wq_w': Wq_w, 'Wq_b': Wq_b, 'Wk_w': Wk_w, 'Wk_b': Wk_b, 'Wv_w': Wv_w, 'Wv_b': Wv_b}
    _L1_gnn_all = _L1_gnn_setup()
    _L1_gnn_in = {k: v for k, v in _L1_gnn_all.items() if k in ('Wq_w', 'Wq_b', 'Wk_w', 'Wk_b', 'Wv_w', 'Wv_b')}
    del _L1_gnn_all

    def _L2_gnn_setup():
        import jax, jax.numpy as jnp
        import numpy as np
        B, N, D_IN, D_OUT = (4, 2048, 256, 256)
        key = jax.random.key(seed)
        k1, k2, k3, k4 = jax.random.split(key, 4)
        x = jax.random.normal(k1, (B, N, D_IN), dtype=jnp.float32)
        A_shape = jax.random.uniform(k2, (B, N, N), dtype=jnp.float32)
        w = jax.random.normal(k3, (D_IN, D_OUT), dtype=jnp.float32)
        a = jax.random.normal(k4, (D_OUT,), dtype=jnp.float32)
        return {'x': x, 'A_shape': A_shape, 'w': w, 'a': a}
    _L2_gnn_all = _L2_gnn_setup()
    _L2_gnn_in = {k: v for k, v in _L2_gnn_all.items() if k in ('w', 'a')}
    del _L2_gnn_all

    def _L3_gnn_setup():
        import jax, jax.numpy as jnp
        import numpy as np
        EPS_LN = 1e-05

        def hypergraph_conv(x, adj, W, b):
            N, C, _ = adj.shape
            H = (adj != 0).astype(x.dtype)
            w = adj.reshape(N, -1)[:, :C]
            xw = jnp.einsum('ncd,hd->nch', x, W)
            Dn = jnp.einsum('nce,ne->nc', H, w)
            Dn = jnp.where(Dn > 0, 1.0 / Dn, 0.0)
            Be = H.sum(axis=1)
            Be = jnp.where(Be > 0, 1.0 / Be, 0.0)
            m = Be[:, :, None] * jnp.einsum('nce,nch->neh', H, xw)
            out = Dn[:, :, None] * jnp.einsum('nce,neh->nch', H, m)
            return out + b

        def layer_norm(x, g, b):
            mu = jnp.mean(x, axis=-1, keepdims=True)
            var = jnp.var(x, axis=-1, keepdims=True)
            return (x - mu) * jax.lax.rsqrt(var + EPS_LN) * g + b
        key = jax.random.key(seed)
        ks = jax.random.split(key, 4)
        N, C, Din, Dh, Dout = (16, 512, 256, 512, 256)
        x = jax.random.normal(ks[0], (N, C, Din), dtype=jnp.float32)
        adj = jax.random.uniform(ks[1], (N, C, C), dtype=jnp.float32, minval=0.1, maxval=1.0)
        W1 = jax.random.normal(ks[2], (Dh, Din), dtype=jnp.float32) * (1.0 / np.sqrt(Din))
        b1 = jnp.zeros((Dh,), dtype=jnp.float32)
        gamma = jnp.ones((Dh,), dtype=jnp.float32)
        beta = jnp.zeros((Dh,), dtype=jnp.float32)
        W2 = jax.random.normal(ks[3], (Dout, Dh), dtype=jnp.float32) * (1.0 / np.sqrt(Dh))
        b2 = jnp.zeros((Dout,), dtype=jnp.float32)
        return {'x': x, 'adj': adj, 'W1': W1, 'b1': b1, 'gamma': gamma, 'beta': beta, 'W2': W2, 'b2': b2}
    _L3_gnn_all = _L3_gnn_setup()
    _L3_gnn_in = {k: v for k, v in _L3_gnn_all.items() if k in ('W1', 'b1', 'gamma', 'beta', 'W2', 'b2')}
    del _L3_gnn_all
    return {'x': x, 'adj': adj, 'nodemask': nodemask, 'L0_gnn_Wqk': _L0_gnn_in['Wqk'], 'L0_gnn_Wv': _L0_gnn_in['Wv'], 'L1_gnn_Wq_w': _L1_gnn_in['Wq_w'], 'L1_gnn_Wq_b': _L1_gnn_in['Wq_b'], 'L1_gnn_Wk_w': _L1_gnn_in['Wk_w'], 'L1_gnn_Wk_b': _L1_gnn_in['Wk_b'], 'L1_gnn_Wv_w': _L1_gnn_in['Wv_w'], 'L1_gnn_Wv_b': _L1_gnn_in['Wv_b'], 'L2_gnn_w': _L2_gnn_in['w'], 'L2_gnn_a': _L2_gnn_in['a'], 'L3_gnn_W1': _L3_gnn_in['W1'], 'L3_gnn_b1': _L3_gnn_in['b1'], 'L3_gnn_gamma': _L3_gnn_in['gamma'], 'L3_gnn_beta': _L3_gnn_in['beta'], 'L3_gnn_W2': _L3_gnn_in['W2'], 'L3_gnn_b2': _L3_gnn_in['b2']}

def reference(x, adj, nodemask, L0_gnn_Wqk, L0_gnn_Wv, L1_gnn_Wq_w, L1_gnn_Wq_b, L1_gnn_Wk_w, L1_gnn_Wk_b, L1_gnn_Wv_w, L1_gnn_Wv_b, L2_gnn_w, L2_gnn_a, L3_gnn_W1, L3_gnn_b1, L3_gnn_gamma, L3_gnn_beta, L3_gnn_W2, L3_gnn_b2):
    import jax
    import jax.numpy as jnp

    def _L0_gnn_ref(X, adj, mask, Wqk, Wv):
        import jax, jax.numpy as jnp
        import numpy as np
        B, N, IN_DIM, ATT_DIM = (2, 4096, 256, 256)
        qk = X @ Wqk
        q, k = jnp.split(qk, 2, axis=-1)
        v = X @ Wv
        att_dim = q.shape[-1]
        inv_scale = 1.0 / jnp.sqrt(jnp.float32(att_dim))
        k_m = k * mask[:, :, None]
        agg = jnp.einsum('bij,bjd->bid', adj, k_m)
        w = inv_scale * mask * jnp.einsum('bid,bid->bi', q, agg)
        L = jax.nn.softmax(w, axis=1)[:, :, None] * v
        return L

    def _L1_gnn_ref(x, adj, Wq_w, Wq_b, Wk_w, Wk_b, Wv_w, Wv_b):
        import jax, jax.numpy as jnp
        import numpy as np
        B, N, D = (8, 1024, 256)
        query = jnp.einsum('bnd,od->bno', x, Wq_w) + Wq_b
        keyt = jnp.einsum('bnd,od->bno', x, Wk_w) + Wk_b
        value = jnp.einsum('bnd,od->bno', x, Wv_w) + Wv_b
        weight = jnp.einsum('bqd,bkd->bqk', query, keyt)
        weight = adj * jnp.exp(weight)
        weight = weight / jnp.sum(weight, axis=2, keepdims=True)
        return jnp.einsum('bqk,bkd->bqd', weight, value)

    def _L2_gnn_ref(x, A_shape, w, a):
        import jax, jax.numpy as jnp
        import numpy as np
        B, N, D_IN, D_OUT = (4, 2048, 256, 256)
        y = x @ w
        s = y @ a
        A = s[..., :, None] + s[..., None, :]
        A = jnp.tanh(A / 8.0) * 8.0
        A = jnp.where(A >= 0, A, 0.1 * A)
        A = jnp.exp(A) * A_shape
        A = A / jnp.sum(A, axis=-1, keepdims=True)
        A = A * jnp.sum(A_shape, axis=-1, keepdims=True)
        out = A @ x @ w
        return out

    def _L3_gnn_ref(x, adj, W1, b1, gamma, beta, W2, b2):
        import jax, jax.numpy as jnp
        import numpy as np
        EPS_LN = 1e-05

        def hypergraph_conv(x, adj, W, b):
            N, C, _ = adj.shape
            H = (adj != 0).astype(x.dtype)
            w = adj.reshape(N, -1)[:, :C]
            xw = jnp.einsum('ncd,hd->nch', x, W)
            Dn = jnp.einsum('nce,ne->nc', H, w)
            Dn = jnp.where(Dn > 0, 1.0 / Dn, 0.0)
            Be = H.sum(axis=1)
            Be = jnp.where(Be > 0, 1.0 / Be, 0.0)
            m = Be[:, :, None] * jnp.einsum('nce,nch->neh', H, xw)
            out = Dn[:, :, None] * jnp.einsum('nce,neh->nch', H, m)
            return out + b

        def layer_norm(x, g, b):
            mu = jnp.mean(x, axis=-1, keepdims=True)
            var = jnp.var(x, axis=-1, keepdims=True)
            return (x - mu) * jax.lax.rsqrt(var + EPS_LN) * g + b
        h = jax.nn.relu(hypergraph_conv(x, adj, W1, b1))
        h = layer_norm(h, gamma, beta)
        y = hypergraph_conv(h, adj, W2, b2)
        return y + x
    h = jnp.maximum(_layernorm(x, axis=-1), 0.0)
    x = x + _L0_gnn_ref(h, adj, nodemask, L0_gnn_Wqk, L0_gnn_Wv)
    h = jnp.maximum(_layernorm(x, axis=-1), 0.0)
    x = x + _L1_gnn_ref(h, adj, L1_gnn_Wq_w, L1_gnn_Wq_b, L1_gnn_Wk_w, L1_gnn_Wk_b, L1_gnn_Wv_w, L1_gnn_Wv_b)
    h = jnp.maximum(_layernorm(x, axis=-1), 0.0)
    x = x + _L2_gnn_ref(h, adj, L2_gnn_w, L2_gnn_a)
    h = jnp.maximum(_layernorm(x, axis=-1), 0.0)
    x = x + _L3_gnn_ref(h, adj, L3_gnn_W1, L3_gnn_b1, L3_gnn_gamma, L3_gnn_beta, L3_gnn_W2, L3_gnn_b2)
    return x

_drawn_inputs = setup_inputs


def setup_inputs(seed=0):
    import zlib

    import numpy as np

    out = dict(_drawn_inputs(seed))
    spreads = {'L1_gnn_Wq_b': (0.0, 0.294),
     'L1_gnn_Wk_b': (0.0, 2.0),
     'L1_gnn_Wv_b': (0.0, 0.1),
     'L3_gnn_b1': (0.0, 2.0),
     'L3_gnn_gamma': (1.0, 0.6),
     'L3_gnn_beta': (0.0, 0.667),
     'L3_gnn_b2': (0.0, 2.0)}
    factors = {'L0_gnn_Wqk': 3.655, 'L0_gnn_Wv': 3.891}
    for name, (base, spread) in spreads.items():
        noise = np.random.default_rng([zlib.crc32(name.encode()), seed]).standard_normal(out[name].shape)
        drawn = base * np.exp(spread * noise) if base else spread * noise
        out[name] = jnp.asarray(drawn.astype(out[name].dtype))
    for name, factor in factors.items():
        out[name] = (out[name] * factor).astype(out[name].dtype)
    return out
```

```python
from contextlib import ExitStack

import concourse.bass as bass
from concourse import mybir

F32 = mybir.dt.float32
F32R = mybir.dt.float32r
ALU = mybir.AluOpType
ACT = mybir.ActivationFunctionType
AX_X = mybir.AxisListType.X

P = 128
PAIR = 2
EPS = 1e-5
TINY = 1.2e-38
LAST_OFF = 4


def build(nc, x, adj, mask, wqk0, wv0, wq1, bq1, wk1, bk1, wv1, bv1, w2, a2, w31, b31, gamma, beta,
          w32, b32, out):
    B, N, D = x.shape
    NG = B // PAIR
    C = D // P
    DH = w31.shape[0]
    K = DH // P
    assert N == P and C == 2 and K == 4
    INV = float(D) ** -0.5

    with ExitStack() as ctx:
        def sb(name, shape, dt=F32):
            return ctx.enter_context(nc.sbuf_tensor(name, shape, dt))

        def sem(name):
            return ctx.enter_context(nc.semaphore(name))

        bank = [ctx.enter_context(nc.psum_tensor(f"bank{i}", [P, 512], F32)) for i in range(8)]

        def quarters(b):
            return bank[b][:, :].rearrange("p (c b n) -> p c b n", c=2, b=2)

        def halves(b):
            return bank[b][:, :].rearrange("p (b d) -> p b d", b=2)

        def small(b):
            return bank[b][:, 0:256].rearrange("p (b d) -> p b d", b=2)

        ident = sb("ident", [P, P])
        rwqk0, rwv0 = sb("rwqk0", [P, C, 2 * D]), sb("rwv0", [P, C, D])
        rwq1, rwk1, rwv1 = sb("rwq1", [P, C, D]), sb("rwk1", [P, C, D]), sb("rwv1", [P, C, D])
        rw2, rw31, rw32 = sb("rw2", [P, C, D]), sb("rw31", [P, K, D]), sb("rw32", [P, C, DH])
        bq_col, bk_col, a_col = sb("bq_col", [P, C]), sb("bk_col", [P, C]), sb("a_col", [P, C])
        gamma_col, beta_col = sb("gamma_col", [P, K]), sb("beta_col", [P, K])
        bv_bc, b1_bc, b2_bc = sb("bv_bc", [P, D]), sb("b1_bc", [P, DH]), sb("b2_bc", [P, D])
        ones = sb("ones", [P, P])
        a_rep, beta_rep = sb("a_rep", [P, C, P]), sb("beta_rep", [P, K, P])
        bq_rep = sb("bq_rep", [P, C, P])
        wq0_t, wk0_t, wv1_t, w2_t = (sb(n, [P, C, D]) for n in ("wq0_t", "wk0_t", "wv1_t", "w2_t"))
        w31_t, w32_t, w32_g = sb("w31_t", [P, C, DH]), sb("w32_t", [P, K, D]), sb("w32_g", [P, K, D])
        m0, m1 = sb("m0", [P, C, D]), sb("m1", [P, C, D])
        wa = sb("wa", [P, C, P])
        vecs = sb("vecs", [P, 5])
        bw2 = sb("bw2", [P, D])
        ubias, rvec, rconst = vecs[:, 0:2], vecs[:, 2:4], vecs[:, 4:5]

        def parts(name, shape):
            return sb(name + "_hi", shape, F32R), sb(name + "_lo", shape, F32R)

        m0_p, m1_p, wv0_p, wv1_p, w2_p = (parts(n, [P, C, D]) for n in ("pm0", "pm1", "pwv0", "pwv1", "pw2"))
        wa_p = parts("pwa", [P, C, P])
        w31_p, w32_p = parts("pw31", [P, C, DH]), parts("pw32", [P, K, D])

        x_in = sb("x_in", [P, PAIR, D])
        X = [sb(f"X{l}", [P, PAIR, D]) for l in range(4)]
        x_out = sb("x_out", [P, PAIR, D])
        XN = [sb(f"XN{l}", [P, PAIR, D]) for l in range(4)]
        h3 = sb("h3", [P, PAIR, D])
        stats = [sb(f"stats{l}", [P, PAIR, 6]) for l in range(5)]
        mv = [sb(f"mv{l}", [P, PAIR, 2]) for l in range(5)]
        vare = [sb(f"vare{l}", [P, PAIR, 1]) for l in range(5)]
        rstd = [sb(f"rstd{l}", [P, PAIR, 1]) for l in range(5)]
        nmr = sb("nmr", [P, PAIR, 1])
        nmr_t = sb("nmr_t", [P, PAIR, 1])
        eps_t, half_t, neg_t = sb("eps_t", [P, PAIR, 1]), sb("half_t", [P, PAIR, 1]), sb("neg_t", [P, PAIR, 1])
        pool_scratch, dve_scratch = sb("pool_scratch", [P, 1]), sb("dve_scratch", [P, 1])
        hT_hi = [sb(f"hT{l}_hi", [P, C, PAIR, P], F32R) for l in range(3)]
        hT_lo = [sb(f"hT{l}_lo", [P, C, PAIR, P], F32R) for l in range(3)]
        hT = [sb(f"hT{l}", [P, C, PAIR, P]) for l in range(2)]
        AD = [sb(f"AD{l}", [P, PAIR, P]) for l in range(4)]
        mask_bc = sb("mask_bc", [P, PAIR, P])
        mask_rows = sb("mask_rows", [PAIR, P])
        adm = sb("adm", [P, PAIR, P])
        tT, uT = sb("tT", [P, C, PAIR, P]), sb("uT", [P, C, PAIR, P])
        junk, junk0 = sb("junk", [P, PAIR, P]), sb("junk0", [P, PAIR, P])
        w0 = sb("w0", [P, PAIR])
        wrow, erow, prow = (sb(n, [PAIR, P]) for n in ("wrow", "erow", "prow"))
        nmax, esum, einv = (sb(n, [PAIR, 1]) for n in ("nmax", "esum", "einv"))
        soft = sb("soft", [P, PAIR])
        r1 = sb("r1", [P, PAIR])
        e1, p1, p1T = sb("e1", [P, PAIR, P]), sb("p1", [P, PAIR, P]), sb("p1T", [P, PAIR, P])
        v1, xv1 = sb("v1", [P, PAIR, D]), sb("xv1", [P, PAIR, D])
        sum1, inv1 = sb("sum1", [P, PAIR]), sb("inv1", [P, PAIR])
        s2 = sb("s2", [P, PAIR])
        th2, lr2, e2 = (sb(n, [P, PAIR, P]) for n in ("th2", "lr2", "e2"))
        a2m, a2T = sb("a2m", [P, PAIR, P]), sb("a2T", [P, PAIR, P])
        sum2, inv2, asum2, ratio2 = (sb(n, [P, PAIR]) for n in ("sum2", "inv2", "asum2", "ratio2"))
        y2 = sb("y2", [P, PAIR, D])
        HT, bHT, G = sb("HT", [P, PAIR, P]), sb("bHT", [P, PAIR, P]), sb("G", [P, PAIR, P])
        wcol = sb("wcol", [P, PAIR])
        cnt, cnt1, binv = (sb(n, [P, PAIR]) for n in ("cnt", "cnt1", "binv"))
        deg, deg1, dinv, Dn = (sb(n, [P, PAIR]) for n in ("deg", "deg1", "dinv", "Dn"))
        aggT_hi, aggT_lo = parts("aggT", [P, C, PAIR, P])
        o1, r3, h1n = (sb(n, [P, PAIR, DH]) for n in ("o1", "r3", "h1n"))
        h1T_hi, h1T_lo = parts("h1T", [P, PAIR, K, P])
        z = sb("z", [P, PAIR, D])
        xb3a, xb3 = sb("xb3a", [P, PAIR, D]), sb("xb3", [P, PAIR, D])

        s_w_loaded = sem("s_w_loaded")
        s_b_loaded = sem("s_b_loaded")
        s_ident_made = sem("s_ident_made")
        s_reps_made = sem("s_reps_made")
        s_consts = sem("s_consts")
        s_wturned = sem("s_wturned")
        s_turned_out = sem("s_turned_out")
        s_hi_done = sem("s_hi_done")
        s_split_done = sem("s_split_done")
        s_x_loaded = sem("s_x_loaded")
        s_x_stored = sem("s_x_stored")
        s_mbc_loaded = sem("s_mbc_loaded")
        s_mrow_loaded = sem("s_mrow_loaded")
        s_a0_loaded = sem("s_a0_loaded")
        s_a1_loaded = sem("s_a1_loaded")
        s_a2_loaded = sem("s_a2_loaded")
        s_a3_loaded = sem("s_a3_loaded")
        s_nmr_raw = sem("s_nmr_raw")
        s_nmr_made = sem("s_nmr_made")
        s_h3_made = sem("s_h3_made")
        s_x0_copied = sem("s_x0_copied")
        s_adm_made = sem("s_adm_made")
        s_tT_mm = sem("s_tT_mm")
        s_tT_out = sem("s_tT_out")
        s_S0_mm = sem("s_S0_mm")
        s_w0_made = sem("s_w0_made")
        s_wT_mm = sem("s_wT_mm")
        s_wrow_made = sem("s_wrow_made")
        s_nmax_made = sem("s_nmax_made")
        s_erow_made = sem("s_erow_made")
        s_einv_made = sem("s_einv_made")
        s_prow_made = sem("s_prow_made")
        s_soft_mm = sem("s_soft_mm")
        s_soft_out = sem("s_soft_out")
        s_V0_mm = sem("s_V0_mm")
        s_uT_mm = sem("s_uT_mm")
        s_uT_out = sem("s_uT_out")
        s_r1_mm = sem("s_r1_mm")
        s_r1_out = sem("s_r1_out")
        s_S1_mm = sem("s_S1_mm")
        s_e1_made = sem("s_e1_made")
        s_p1_made = sem("s_p1_made")
        s_inv1_made = sem("s_inv1_made")
        s_PT_mm = sem("s_PT_mm")
        s_PT_out = sem("s_PT_out")
        s_V1_mm = sem("s_V1_mm")
        s_V1_out = sem("s_V1_out")
        s_PV_mm = sem("s_PV_mm")
        s_xv1_made = sem("s_xv1_made")
        s_sb_mm = sem("s_sb_mm")
        s_s2_made = sem("s_s2_made")
        s_tanh_made = sem("s_tanh_made")
        s_lr_made = sem("s_lr_made")
        s_e2_made = sem("s_e2_made")
        s_a2_made = sem("s_a2_made")
        s_inv2_made = sem("s_inv2_made")
        s_asum_made = sem("s_asum_made")
        s_ratio_made = sem("s_ratio_made")
        s_AT_mm = sem("s_AT_mm")
        s_AT_out = sem("s_AT_out")
        s_y_mm = sem("s_y_mm")
        s_y_out = sem("s_y_out")
        s_Ay_mm = sem("s_Ay_mm")
        s_AdT_mm = sem("s_AdT_mm")
        s_HT_made = sem("s_HT_made")
        s_cnt1_made = sem("s_cnt1_made")
        s_binv_made = sem("s_binv_made")
        s_bHT_made = sem("s_bHT_made")
        s_wcol_made = sem("s_wcol_made")
        s_deg_mm = sem("s_deg_mm")
        s_deg_out = sem("s_deg_out")
        s_deg1_made = sem("s_deg1_made")
        s_dinv_made = sem("s_dinv_made")
        s_Dn_made = sem("s_Dn_made")
        s_G_mm = sem("s_G_mm")
        s_G_out = sem("s_G_out")
        s_agg_mm = sem("s_agg_mm")
        s_agg_hi = sem("s_agg_hi")
        s_agg_lo = sem("s_agg_lo")
        s_O1_mm = sem("s_O1_mm")
        s_o1_made = sem("s_o1_made")
        s_r3_made = sem("s_r3_made")
        s_h1n_made = sem("s_h1n_made")
        s_h1T_mm = sem("s_h1T_mm")
        s_h1T_hi = sem("s_h1T_hi")
        s_h1T_lo = sem("s_h1T_lo")
        s_z_mm = sem("s_z_mm")
        s_z_out = sem("s_z_out")
        s_Gz_mm = sem("s_Gz_mm")
        s_xb3a_made = sem("s_xb3a_made")
        s_xb3_made = sem("s_xb3_made")
        s_stats = [sem(f"s_stats{l}") for l in range(5)]
        s_mv = [sem(f"s_mv{l}") for l in range(5)]
        s_vare = [sem(f"s_vare{l}") for l in range(5)]
        s_rstd = [sem(f"s_rstd{l}") for l in range(5)]
        s_xn = [sem(f"s_xn{l}") for l in range(4)]
        s_turned = [sem(f"s_turned{l}") for l in range(3)]
        s_hi = [sem(f"s_hi{l}") for l in range(3)]
        s_lo = [sem(f"s_lo{l}") for l in range(3)]
        s_full = [sem(f"s_full{l}") for l in range(2)]
        s_final = [sem(f"s_final{l}") for l in range(4)]

        def upto(n, unit=1):
            return (min(max(n, 0), NG) if isinstance(n, int) else n) * unit

        turn_jobs = [(wq0_t[:, :, :], 512), (wk0_t[:, :, :], 512), (wv1_t[:, :, :], 512), (w2_t[:, :, :], 512),
                     (w31_t[:, 0, :], 512), (w31_t[:, 1, :], 512), (0, "gamma"), (2, "gamma"),
                     (m0[:, :, :], 512), (m1[:, :, :], 512), (wa[:, :, :], 256), (vecs[:, :], 5), (bw2[:, :], 256)]
        TURNS = len(turn_jobs)
        splits = [(m0, m0_p), (m1, m1_p), (rwv0, wv0_p), (wv1_t, wv1_p), (rw2, w2_p), (wa, wa_p),
                  (w31_t, w31_p), (w32_g, w32_p)]
        TBANK = [6, 1, 2]

        FIRST, LAST = LAST_OFF + 1, NG - 2

        def steps(eng, step):
            for t in range(-1, FIRST):
                step(t, lambda off, t=t: 0 <= t - off < NG)
            with eng.Fori(FIRST, LAST + 1) as t:
                step(t, lambda off: True)
            for t in range(LAST + 1, NG + LAST_OFF):
                step(t, lambda off, t=t: 0 <= t - off < NG)

        block = ctx.enter_context(nc.Block())

        def col(v):
            return v.rearrange("(c p) -> p c", p=P)

        @block.sync
        def _(sp):
            big = [(rwqk0, wqk0), (rwv0, wv0), (rwq1, wq1), (rwk1, wk1), (rwv1, wv1), (rw2, w2),
                   (rw31, w31), (rw32, w32)]
            for dst, src in big:
                sp.dma_start(dst[:, :, :], src.rearrange("(c p) n -> p c n", p=P)).then_inc(s_w_loaded, 16)

            def rows(v, g):
                return v[bass.ds(g * PAIR, PAIR)] if not isinstance(g, int) else v[g * PAIR:(g + 1) * PAIR]

            def load(dst, src, g, signal, free, n):
                sp.wait_ge(free, upto(n))
                sp.dma_start(dst[:, :, :], rows(src, g).rearrange("b p d -> p b d")).then_inc(signal, 16)

            def step(t, live):
                if live(-1):
                    if isinstance(t, int) and t == -1:
                        load(x_in, x, 0, s_x_loaded, s_x0_copied, 0)
                if live(0):
                    load(AD[0], adj, t, s_a0_loaded, s_adm_made, t)
                    sp.wait_ge(s_adm_made, upto(t))
                    g = t
                    mrows = rows(mask, g)
                    sp.dma_start(mask_bc[:, :, :], mrows.unsqueeze(0).broadcast_to([P, PAIR, P])
                                 ).then_inc(s_mbc_loaded, 16)
                    sp.wait_ge(s_wrow_made, upto(t))
                    sp.dma_start(mask_rows[:, :], mrows).then_inc(s_mrow_loaded, 16)
                if live(1):
                    load(AD[1], adj, t - 1, s_a1_loaded, s_p1_made, t - 1)
                if live(2):
                    load(AD[2], adj, t - 2, s_a2_loaded, s_a2_made, t - 2)
                if live(3):
                    load(AD[3], adj, t - 3, s_a3_loaded, s_AdT_mm, t - 3)
                if live(0) and live(-1):
                    load(x_in, x, t + 1, s_x_loaded, s_x0_copied, t + 1)

            steps(sp, step)

        @block.gpsimd
        def _(pool):
            gp = nc.gpsimd
            gp.memset(ident[:, :], 0.0).then_inc(s_consts, 1)
            gp.memset(ones[:, :], 1.0)
            gp.memset(eps_t[:, :, :], EPS)
            gp.memset(half_t[:, :, :], -0.5)
            gp.memset(pool_scratch[:, :], 0.0)
            gp.memset(neg_t[:, :, :], -1.0).then_inc(s_consts, 1)
            pool.wait_ge(s_consts, 2)
            gp.affine_select(out=ident[:, :], in_=ident[:, :], compare_op=ALU.not_equal, fill=1.0,
                             base=0, pattern=[[-1, P]], channel_multiplier=1).then_inc(s_ident_made, 1)
            pool.wait_ge(s_b_loaded, 16 * 8)
            for c in range(C):
                gp.tensor_scalar(a_rep[:, c, :], ones[:, :], a_col[:, c:c + 1], None, ALU.mult)
                gp.tensor_scalar(bq_rep[:, c, :], ones[:, :], bq_col[:, c:c + 1], None, ALU.mult)
            for k in range(K):
                last = gp.tensor_scalar(beta_rep[:, k, :], ones[:, :], beta_col[:, k:k + 1], None, ALU.mult)
            last.then_inc(s_reps_made, 1)

            def rstd_of(l, n):
                pool.wait_ge(s_mv[l], upto(n))
                gp.tensor_tensor(vare[l][:, :, :], mv[l][:, :, 1:2], eps_t[:, :, :], ALU.add
                                 ).then_inc(s_vare[l], 1)
                pool.wait_ge(s_vare[l], upto(n))
                gp.tensor_tensor(rstd[l][:, :, :], vare[l][:, :, :], half_t[:, :, :], ALU.pow
                                 ).then_inc(s_rstd[l], 1)

            def normalise(l, n, src, used):
                rstd_of(l, n)
                pool.wait_ge(used, upto(n - 1))
                pool.wait_ge(s_rstd[l], upto(n))
                gp.tensor_tensor(pool_scratch[:, :], eps_t[:, 0, :], half_t[:, 0, :], ALU.add)
                for b in range(PAIR):
                    last = gp.tensor_scalar(XN[l][:, b, :], src[:, b, :], mv[l][:, b, 0:1],
                                            rstd[l][:, b, 0:1], ALU.subtract, ALU.mult)
                last.then_inc(s_xn[l], 1)

            def bc(v):
                return v[:, :].unsqueeze(1).broadcast_to([P, PAIR, D])

            def step(t, live):
                if live(4):
                    rstd_of(4, t - 3)
                    pool.wait_ge(s_rstd[4], upto(t - 3))
                    pool.wait_ge(s_h1n_made, upto(t - 4))
                    gp.tensor_tensor(nmr_t[:, :, :], mv[4][:, :, 0:1], rstd[4][:, :, :], ALU.mult
                                     ).then_inc(s_nmr_raw, 1)
                    pool.wait_ge(s_nmr_raw, upto(t - 3))
                    gp.tensor_tensor(nmr[:, :, :], nmr_t[:, :, :], neg_t[:, :, :], ALU.mult
                                     ).then_inc(s_nmr_made, 1)
                if live(1):
                    pool.wait_ge(s_lo[1], upto(t))
                    pool.wait_ge(s_S1_mm, upto(t - 1))
                    gp.tensor_tensor(hT[1][:, :, :, :], hT_hi[1][:, :, :, :].bitcast(F32),
                                     hT_lo[1][:, :, :, :].bitcast(F32), ALU.add).then_inc(s_full[1], 1)
                    pool.wait_ge(s_final[0], upto(t))
                    pool.wait_ge(s_final[1], upto(t - 1))
                    gp.tensor_tensor(xv1[:, :, :], X[1][:, :, :], bc(bv_bc), ALU.add).then_inc(s_xv1_made, 1)
                if live(0):
                    pool.wait_ge(s_x_loaded, upto(t + 1, 16))
                    pool.wait_ge(s_final[0], upto(t))
                    pool.wait_ge(s_xn[0], upto(t + 1))
                    gp.tensor_tensor(pool_scratch[:, :], eps_t[:, 0, :], half_t[:, 0, :], ALU.add)
                    gp.tensor_copy(X[0][:, :, :], x_in[:, :, :]).then_inc(s_x0_copied, 1)
                    pool.wait_ge(s_lo[0], upto(t + 1))
                    pool.wait_ge(s_S0_mm, upto(t))
                    gp.tensor_tensor(hT[0][:, :, :, :], hT_hi[0][:, :, :, :].bitcast(F32),
                                     hT_lo[0][:, :, :, :].bitcast(F32), ALU.add).then_inc(s_full[0], 1)
                    pool.wait_ge(s_a0_loaded, upto(t + 1, 16))
                    pool.wait_ge(s_mbc_loaded, upto(t + 1, 16))
                    pool.wait_ge(s_w0_made, upto(t))
                    gp.tensor_tensor(adm[:, :, :], AD[0][:, :, :], mask_bc[:, :, :], ALU.mult
                                     ).then_inc(s_adm_made, 1)
                if live(3):
                    pool.wait_ge(s_xn[3], upto(t - 2))
                    gp.tensor_tensor(xb3a[:, :, :], X[3][:, :, :], bc(b2_bc), ALU.add).then_inc(s_xb3a_made, 1)
                    pool.wait_ge(s_xb3a_made, upto(t - 2))
                    pool.wait_ge(s_h3_made, upto(t - 2))
                    pool.wait_ge(s_final[3], upto(t - 3))
                    gp.tensor_tensor(xb3[:, :, :], xb3a[:, :, :], h3[:, :, :], ALU.add).then_inc(s_xb3_made, 1)
                if live(2):
                    normalise(3, t - 1, X[3], s_h3_made)
                if live(1):
                    normalise(2, t, X[2], s_turned[2])
                if live(-1):
                    pool.wait_ge(s_x_loaded, upto(t + 2, 16))
                    normalise(0, t + 2, x_in, s_turned[0])
                if live(0):
                    normalise(1, t + 1, X[1], s_turned[1])

            steps(pool, step)

        @block.scalar
        def _(act):
            sc = nc.scalar
            vec = [(bq_col, col(bq1)), (bk_col, col(bk1)), (a_col, col(a2)), (gamma_col, col(gamma)),
                   (beta_col, col(beta)), (bv_bc, bv1.unsqueeze(0).broadcast_to([P, D])),
                   (b1_bc, b31.unsqueeze(0).broadcast_to([P, DH])), (b2_bc, b32.unsqueeze(0).broadcast_to([P, D]))]
            for dst, src in vec:
                act.dma_start(dst[:, :], src, allow_slow_non_contiguous=True).then_inc(s_b_loaded, 16)
            act.wait_ge(s_w_loaded, 16 * 8)
            act.wait_ge(s_turned_out, TURNS)
            for whole, (hi, lo) in splits:
                last = sc.activation(hi[:, :, :], whole[:, :, :], ACT.Copy)
            last.then_inc(s_hi_done, 1)

            def store(g):
                dst = out[g * PAIR:(g + 1) * PAIR] if isinstance(g, int) else out[bass.ds(g * PAIR, PAIR)]
                act.dma_start(dst.rearrange("b p d -> p b d"), x_out[:, :, :]).then_inc(s_x_stored, 16)

            def high(l, n):
                act.wait_ge(s_turned[l], upto(n))
                act.wait_ge((s_V0_mm, s_V1_mm, s_y_mm)[l], upto(n - 1))
                if l < 2:
                    act.wait_ge(s_full[l], upto(n - 1))
                act.wait_ge(s_lo[l], upto(n - 1))
                sc.activation(hT_hi[l][:, :, :, :], quarters(TBANK[l]), ACT.Relu).then_inc(s_hi[l], 1)

            def step(t, live):
                if live(1):
                    high(1, t)
                if live(2):
                    act.wait_ge(s_s2_made, upto(t - 1))
                    act.wait_ge(s_lr_made, upto(t - 2))
                    for b in range(PAIR):
                        last = sc.activation(th2[:, b, :], small(0)[:, b, :], ACT.Tanh,
                                             bias=s2[:, b:b + 1], scale=0.125)
                    last.then_inc(s_tanh_made, 1)
                if live(4):
                    act.wait_ge(s_nmr_made, upto(t - 3))
                    act.wait_ge(s_h1T_mm, upto(t - 4))
                    for b in range(PAIR):
                        last = sc.activation(h1n[:, b, :], r3[:, b, :], ACT.Identity,
                                             bias=nmr[:, b, 0:1], scale=rstd[4][:, b, 0:1])
                    last.then_inc(s_h1n_made, 1)
                if live(2):
                    act.wait_ge(s_y_mm, upto(t - 1))
                    act.wait_ge(s_Ay_mm, upto(t - 2))
                    sc.activation(y2[:, :, :], halves(2), ACT.Copy).then_inc(s_y_out, 1)
                    act.wait_ge(s_lr_made, upto(t - 1))
                    act.wait_ge(s_a2_made, upto(t - 2))
                    sc.activation(e2[:, :, :], lr2[:, :, :], ACT.Exp, scale=8.0).then_inc(s_e2_made, 1)
                if live(1):
                    act.wait_ge(s_uT_mm, upto(t))
                    act.wait_ge(s_S1_mm, upto(t - 1))
                    for m in range(C):
                        last = sc.activation(uT[:, m, :, :], quarters(5)[:, m, :, :], ACT.Identity,
                                             bias=ubias[:, m:m + 1])
                    last.then_inc(s_uT_out, 1)
                if live(0):
                    high(0, t + 1)
                if live(4):
                    act.wait_ge(s_h1T_mm, upto(t - 3))
                    act.wait_ge(s_z_mm, upto(t - 4))
                    act.wait_ge(s_h1T_lo, upto(t - 4))
                    for b in range(PAIR):
                        last = sc.activation(h1T_hi[:, b, :, :], bank[3 + b][:, :].rearrange(
                            "p (k n) -> p k n", k=K), ACT.Copy)
                    last.then_inc(s_h1T_hi, 1)
                if live(1):
                    act.wait_ge(s_S1_mm, upto(t))
                    act.wait_ge(s_r1_out, upto(t))
                    act.wait_ge(s_p1_made, upto(t - 1))
                    for b in range(PAIR):
                        last = sc.activation(e1[:, b, :], small(1)[:, b, :], ACT.Exp, bias=r1[:, b:b + 1])
                    last.then_inc(s_e1_made, 1)
                if live(2):
                    act.wait_ge(s_AT_mm, upto(t - 1))
                    sc.activation(a2T[:, :, :], small(3), ACT.Copy).then_inc(s_AT_out, 1)
                if live(1):
                    act.wait_ge(s_V1_mm, upto(t))
                    act.wait_ge(s_PV_mm, upto(t - 1))
                    sc.activation(v1[:, :, :], halves(2), ACT.Copy).then_inc(s_V1_out, 1)
                if live(0):
                    act.wait_ge(s_tT_mm, upto(t + 1))
                    act.wait_ge(s_S0_mm, upto(t))
                    sc.activation(tT[:, :, :, :], quarters(5), ACT.Copy).then_inc(s_tT_out, 1)
                if live(1):
                    act.wait_ge(s_PT_mm, upto(t))
                    sc.activation(p1T[:, :, :], small(6), ACT.Copy).then_inc(s_PT_out, 1)
                if live(3):
                    act.wait_ge(s_G_mm, upto(t - 2))
                    act.wait_ge(s_Gz_mm, upto(t - 3))
                    sc.activation(G[:, :, :], small(4), ACT.Copy).then_inc(s_G_out, 1)
                if live(0):
                    act.wait_ge(s_nmax_made, upto(t + 1))
                    act.wait_ge(s_prow_made, upto(t))
                    sc.activation(erow[:, :], wrow[:, :], ACT.Exp, bias=nmax[:, :], accum_out=esum[:, :]
                                  ).then_inc(s_erow_made, 1)
                if live(3):
                    act.wait_ge(s_agg_mm, upto(t - 2))
                    act.wait_ge(s_O1_mm, upto((t - 3) * 1))
                    act.wait_ge(s_agg_lo, upto(t - 3))
                    sc.activation(aggT_hi[:, :, :, :], quarters(1), ACT.Copy).then_inc(s_agg_hi, 1)
                if live(2):
                    act.wait_ge(s_xn[3], upto(t - 1))
                    act.wait_ge(s_agg_mm, upto(t - 2))
                    act.wait_ge(s_xb3_made, upto(t - 2))
                    sc.activation(h3[:, :, :], XN[3][:, :, :], ACT.Relu).then_inc(s_h3_made, 1)
                if live(1):
                    high(2, t)
                if live(3):
                    act.wait_ge(s_o1_made, upto(t - 2))
                    act.wait_ge(s_h1n_made, upto(t - 3))
                    sc.activation(r3[:, :, :], o1[:, :, :], ACT.Relu).then_inc(s_r3_made, 1)
                if live(4):
                    act.wait_ge(s_final[3], upto(t - 3))
                    store(t - 4)

            steps(act, step)
            act.wait_ge(s_x_stored, 16 * NG)

        @block.vector
        def _(dve):
            v = nc.vector
            for j in range(len(turn_jobs)):
                dve.wait_ge(s_wturned, j + 1)
                dst, kind = turn_jobs[j]
                src = bank[j % 8]
                if kind == "gamma":
                    dve.wait_ge(s_b_loaded, 16 * 8)
                    k0 = dst
                    v.tensor_copy(w32_t[:, k0:k0 + 2, :], halves(j % 8))
                    for k in range(2):
                        last = v.tensor_scalar(w32_g[:, k0 + k, :], halves(j % 8)[:, k, :],
                                               gamma_col[:, k0 + k:k0 + k + 1], None, ALU.mult)
                    last.then_inc(s_turned_out, 1)
                else:
                    v.tensor_copy(dst, src[:, 0:kind]).then_inc(s_turned_out, 1)
            dve.wait_ge(s_hi_done, 1)
            for whole, (hi, lo) in splits:
                last = v.tensor_tensor(lo[:, :, :], whole[:, :, :], hi[:, :, :].bitcast(F32), ALU.subtract)
            last.then_inc(s_split_done, 1)

            def stats_of(l, n, src):
                dve.wait_ge(s_mv[l], upto(n - 1))
                for b in range(PAIR):
                    last = v.bn_stats(stats[l][:, b, :], src[:, b, :])
                last.then_inc(s_stats[l], 1)

            def aggregate(l, n):
                dve.wait_ge(s_stats[l], upto(n))
                dve.wait_ge(s_xn[l] if l < 4 else s_nmr_made, upto(n - 1))
                v.memset(dve_scratch[:, :], 0.0)
                for b in range(PAIR):
                    last = v.bn_aggr(mv[l][:, b, :], stats[l][:, b, :])
                last.then_inc(s_mv[l], 1)

            def low(l, n):
                dve.wait_ge(s_hi[l], upto(n))
                v.scalar_tensor_tensor(hT_lo[l][:, :, :, :].rearrange("p c b n -> p (c b n)"), bank[TBANK[l]][:, :], 0.0,
                                       hT_hi[l][:, :, :, :].bitcast(F32).rearrange("p c b n -> p (c b n)"),
                                       ALU.max, ALU.subtract).then_inc(s_lo[l], 1)

            def weighted_sum(dst, prod, acc, scale):
                for b in range(PAIR):
                    last = v.tensor_tensor_reduce(out=dst[:, b, :], in0=prod[0][:, b, :], in1=prod[1][:, b, :],
                                                  scale=scale, scalar=0.0, op0=ALU.mult, op1=ALU.add,
                                                  accum_out=acc[:, b:b + 1])
                return last

            def step(t, live):
                if live(2):
                    dve.wait_ge(s_sb_mm, upto(t - 1))
                    dve.wait_ge(s_tanh_made, upto(t - 2))
                    dve.wait_ge(s_s2_made, upto(t - 2))
                    for b in range(PAIR):
                        last = v.tensor_tensor_reduce(out=junk[:, b, :], in0=small(0)[:, b, :], in1=ident[:, :],
                                                      scale=0.125, scalar=0.0, op0=ALU.mult, op1=ALU.add,
                                                      accum_out=s2[:, b:b + 1])
                    last.then_inc(s_s2_made, 1)
                if live(1):
                    low(1, t)
                if live(4):
                    dve.wait_ge(s_r3_made, upto(t - 3))
                    stats_of(4, t - 3, r3)
                    aggregate(4, t - 3)
                if live(2):
                    dve.wait_ge(s_tanh_made, upto(t - 1))
                    dve.wait_ge(s_e2_made, upto(t - 2))
                    v.scalar_tensor_tensor(lr2[:, :, :], th2[:, :, :], 0.1, th2[:, :, :], ALU.mult, ALU.max
                                           ).then_inc(s_lr_made, 1)
                    dve.wait_ge(s_a2_loaded, upto(t - 1, 16))
                    dve.wait_ge(s_ratio_made, upto(t - 2))
                    v.tensor_reduce(asum2[:, :], AD[2][:, :, :], AX_X, ALU.add).then_inc(s_asum_made, 1)
                if live(0):
                    low(0, t + 1)
                if live(2):
                    dve.wait_ge(s_e2_made, upto(t - 1))
                    dve.wait_ge(s_AT_mm, upto(t - 2))
                    dve.wait_ge(s_inv2_made, upto(t - 2))
                    weighted_sum(a2m, (e2, AD[2]), sum2, 1.0).then_inc(s_a2_made, 1)
                if live(4):
                    dve.wait_ge(s_h1T_hi, upto(t - 3))
                    for b in range(PAIR):
                        last = v.tensor_tensor(h1T_lo[:, b, :, :], bank[3 + b][:, :].rearrange(
                            "p (k n) -> p k n", k=K), h1T_hi[:, b, :, :].bitcast(F32), ALU.subtract)
                    last.then_inc(s_h1T_lo, 1)
                if live(2):
                    dve.wait_ge(s_a2_made, upto(t - 1))
                    dve.wait_ge(s_ratio_made, upto(t - 2))
                    v.reciprocal(inv2[:, :], sum2[:, :]).then_inc(s_inv2_made, 1)
                if live(1):
                    dve.wait_ge(s_r1_mm, upto(t))
                    dve.wait_ge(s_e1_made, upto(t - 1))
                    v.tensor_scalar(r1[:, :], bank[7][:, 0:PAIR], rconst, None, ALU.add).then_inc(s_r1_out, 1)
                if live(2):
                    dve.wait_ge(s_inv2_made, upto(t - 1))
                    dve.wait_ge(s_final[2], upto(t - 2))
                    v.tensor_tensor(ratio2[:, :], inv2[:, :], asum2[:, :], ALU.mult).then_inc(s_ratio_made, 1)
                if live(4):
                    dve.wait_ge(s_z_mm, upto(t - 3))
                    dve.wait_ge(s_Gz_mm, upto(t - 4))
                    v.tensor_tensor(z[:, :, :], halves(0), bw2[:, :].unsqueeze(1).broadcast_to([P, PAIR, D]),
                                    ALU.add).then_inc(s_z_out, 1)
                if live(1):
                    dve.wait_ge(s_e1_made, upto(t))
                    dve.wait_ge(s_a1_loaded, upto(t, 16))
                    dve.wait_ge(s_PT_mm, upto(t - 1))
                    dve.wait_ge(s_inv1_made, upto(t - 1))
                    weighted_sum(p1, (e1, AD[1]), sum1, 1.0).then_inc(s_p1_made, 1)
                if live(4):
                    dve.wait_ge(s_Dn_made, upto(t - 3))
                    dve.wait_ge(s_Gz_mm, upto(t - 3))
                    dve.wait_ge(s_xb3_made, upto(t - 3))
                    dve.wait_ge(s_x_stored, upto(t - 4, 16))
                    for b in range(PAIR):
                        last = v.scalar_tensor_tensor(x_out[:, b, :], halves(0)[:, b, :], Dn[:, b:b + 1],
                                                      xb3[:, b, :], ALU.mult, ALU.add)
                    last.then_inc(s_final[3], 1)
                if live(1):
                    dve.wait_ge(s_p1_made, upto(t))
                    dve.wait_ge(s_final[1], upto(t - 1))
                    v.reciprocal(inv1[:, :], sum1[:, :]).then_inc(s_inv1_made, 1)
                if live(0):
                    dve.wait_ge(s_S0_mm, upto(t + 1))
                    dve.wait_ge(s_adm_made, upto(t + 1))
                    dve.wait_ge(s_wT_mm, upto(t))
                    dve.wait_ge(s_w0_made, upto(t))
                    weighted_sum(junk0, (small(1), adm), w0, INV).then_inc(s_w0_made, 1)
                if live(2):
                    dve.wait_ge(s_Ay_mm, upto(t - 1))
                    dve.wait_ge(s_ratio_made, upto(t - 1))
                    dve.wait_ge(s_xb3a_made, upto(t - 2))
                    dve.wait_ge(s_xn[3], upto(t - 2))
                    dve.wait_ge(s_stats[3], upto(t - 2))
                    for b in range(PAIR):
                        last = v.scalar_tensor_tensor(X[3][:, b, :], halves(4)[:, b, :], ratio2[:, b:b + 1],
                                                      X[2][:, b, :], ALU.mult, ALU.add)
                    last.then_inc(s_final[2], 1)
                if live(3):
                    dve.wait_ge(s_AdT_mm, upto(t - 2))
                    dve.wait_ge(s_G_mm, upto(t - 3))
                    dve.wait_ge(s_bHT_made, upto(t - 3))
                    dve.wait_ge(s_cnt1_made, upto(t - 3))
                    for b in range(PAIR):
                        v.tensor_scalar(HT[:, b, :], small(3)[:, b, :], 0.0, 0.0, ALU.not_equal, ALU.add,
                                        accum_out=cnt[:, b:b + 1])
                    v.tensor_copy(wcol[:, :], small(3)[:, :, 0]).then_inc(s_HT_made, 1)
                if live(1):
                    dve.wait_ge(s_inv1_made, upto(t))
                    dve.wait_ge(s_PV_mm, upto(t))
                    dve.wait_ge(s_xv1_made, upto(t))
                    dve.wait_ge(s_xn[2], upto(t - 1))
                    dve.wait_ge(s_final[2], upto(t - 1))
                    for b in range(PAIR):
                        last = v.scalar_tensor_tensor(X[2][:, b, :], halves(2)[:, b, :], inv1[:, b:b + 1],
                                                      xv1[:, b, :], ALU.mult, ALU.add)
                    last.then_inc(s_final[1], 1)
                if live(3):
                    dve.wait_ge(s_HT_made, upto(t - 2))
                    dve.wait_ge(s_binv_made, upto(t - 3))
                    v.tensor_scalar(cnt1[:, :], cnt[:, :], 1.0, None, ALU.max).then_inc(s_cnt1_made, 1)
                if live(1):
                    dve.wait_ge(s_final[1], upto(t))
                    stats_of(2, t, X[2])
                if live(3):
                    dve.wait_ge(s_cnt1_made, upto(t - 2))
                    dve.wait_ge(s_bHT_made, upto(t - 3))
                    v.reciprocal(binv[:, :], cnt1[:, :]).then_inc(s_binv_made, 1)
                if live(1):
                    aggregate(2, t)
                if live(3):
                    dve.wait_ge(s_binv_made, upto(t - 2))
                    for b in range(PAIR):
                        last = v.tensor_scalar(bHT[:, b, :], HT[:, b, :], binv[:, b:b + 1], None, ALU.mult)
                    last.then_inc(s_bHT_made, 1)
                if live(0):
                    dve.wait_ge(s_wT_mm, upto(t + 1))
                    dve.wait_ge(s_mrow_loaded, upto(t + 1, 16))
                    dve.wait_ge(s_erow_made, upto(t))
                    dve.wait_ge(s_nmax_made, upto(t))
                    v.tensor_tensor(wrow[:, :], bank[7][0:PAIR, 0:P], mask_rows[:, :], ALU.mult
                                    ).then_inc(s_wrow_made, 1)
                    dve.wait_ge(s_wrow_made, upto(t + 1))
                    v.tensor_reduce(nmax[:, :], wrow[:, :], AX_X, ALU.max, negate=True).then_inc(s_nmax_made, 1)
                if live(2):
                    dve.wait_ge(s_final[2], upto(t - 1))
                    stats_of(3, t - 1, X[3])
                    aggregate(3, t - 1)
                if live(0):
                    dve.wait_ge(s_prow_made, upto(t))
                    dve.wait_ge(s_erow_made, upto(t + 1))
                    v.reciprocal(einv[:, :], esum[:, :]).then_inc(s_einv_made, 1)
                    dve.wait_ge(s_einv_made, upto(t + 1))
                    dve.wait_ge(s_soft_mm, upto(t))
                    v.tensor_scalar(prow[:, :], erow[:, :], einv[:, :], None, ALU.mult).then_inc(s_prow_made, 1)
                if live(3):
                    dve.wait_ge(s_deg_mm, upto(t - 2))
                    dve.wait_ge(s_Dn_made, upto(t - 3))
                    v.tensor_copy(deg[:, :], bank[6][:, 256:256 + PAIR]).then_inc(s_deg_out, 1)
                    dve.wait_ge(s_deg_out, upto(t - 2))
                    v.tensor_scalar(deg1[:, :], deg[:, :], TINY, None, ALU.max).then_inc(s_deg1_made, 1)
                    dve.wait_ge(s_deg1_made, upto(t - 2))
                    v.reciprocal(dinv[:, :], deg1[:, :]).then_inc(s_dinv_made, 1)
                    dve.wait_ge(s_dinv_made, upto(t - 2))
                    dve.wait_ge(s_final[3], upto(t - 3))
                    dve.wait_ge(s_o1_made, upto(t - 3))
                    v.scalar_tensor_tensor(Dn[:, :], deg[:, :], 0.0, dinv[:, :], ALU.is_gt, ALU.mult
                                           ).then_inc(s_Dn_made, 1)
                    dve.wait_ge(s_agg_hi, upto(t - 2))
                    v.tensor_tensor(aggT_lo[:, :, :, :].rearrange("p c b n -> p (c b n)"), bank[1][:, :],
                                    aggT_hi[:, :, :, :].bitcast(F32).rearrange("p c b n -> p (c b n)"), ALU.subtract
                                    ).then_inc(s_agg_lo, 1)
                if live(0):
                    dve.wait_ge(s_soft_mm, upto(t + 1))
                    dve.wait_ge(s_final[0], upto(t))
                    v.tensor_copy(soft[:, :], bank[7][:, 0:PAIR]).then_inc(s_soft_out, 1)
                    dve.wait_ge(s_soft_out, upto(t + 1))
                    dve.wait_ge(s_V0_mm, upto(t + 1))
                    dve.wait_ge(s_x0_copied, upto(t + 1))
                    dve.wait_ge(s_xv1_made, upto(t))
                    dve.wait_ge(s_xn[1], upto(t))
                    dve.wait_ge(s_stats[1], upto(t))
                    for b in range(PAIR):
                        last = v.scalar_tensor_tensor(X[1][:, b, :], halves(0)[:, b, :], soft[:, b:b + 1],
                                                      X[0][:, b, :], ALU.mult, ALU.add)
                    last.then_inc(s_final[0], 1)
                if live(1):
                    low(2, t)
                if live(0):
                    dve.wait_ge(s_final[0], upto(t + 1))
                    stats_of(1, t + 1, X[1])
                if live(3):
                    dve.wait_ge(s_O1_mm, upto(t - 2))
                    dve.wait_ge(s_Dn_made, upto(t - 2))
                    dve.wait_ge(s_r3_made, upto(t - 3))
                    for b in range(PAIR):
                        last = v.scalar_tensor_tensor(o1[:, b, :], bank[3 + b][:, :], Dn[:, b:b + 1],
                                                      b1_bc[:, :], ALU.mult, ALU.add)
                    last.then_inc(s_o1_made, 1)
                if live(0):
                    aggregate(1, t + 1)
                if live(-1):
                    dve.wait_ge(s_x_loaded, upto(t + 2, 16))
                    stats_of(0, t + 2, x_in)
                    aggregate(0, t + 2)

            steps(dve, step)

        @block.tensor
        def _(pe):
            mm = nc.tensor.matmul

            def turn(dst, src):
                return nc.tensor.transpose(dst, src, ident[:, :])

            def product(dst, terms):
                for i, (a, b) in enumerate(terms):
                    last = mm(dst, a, b, start=(i == 0), stop=(i == len(terms) - 1))
                return last

            def split_product(dst, terms):
                return product(dst, [(x, y) for (ah, al), (bh, bl) in terms
                                     for x, y in ((ah, bl), (al, bh), (ah, bh))])

            pe.wait_ge(s_ident_made, 1)
            pe.wait_ge(s_reps_made, 1)
            pe.wait_ge(s_w_loaded, 16 * 8)
            def blocks(b, src, rows, cols):
                i = 0
                for c in cols:
                    for r in rows:
                        last = turn(bank[b][:, i * P:(i + 1) * P], src[:, r, c * P:(c + 1) * P])
                        i += 1
                return last
            def chunk(c):
                return slice(c * P, (c + 1) * P)
            blocks(0, rwqk0, range(C), range(0, C)).then_inc(s_wturned, 1)
            blocks(1, rwqk0, range(C), range(C, 2 * C)).then_inc(s_wturned, 1)
            blocks(2, rwv1, range(C), range(C)).then_inc(s_wturned, 1)
            blocks(3, rw2, range(C), range(C)).then_inc(s_wturned, 1)
            blocks(4, rw31, range(K), range(0, 1)).then_inc(s_wturned, 1)
            blocks(5, rw31, range(K), range(1, 2)).then_inc(s_wturned, 1)
            blocks(6, rw32, range(C), range(0, 2)).then_inc(s_wturned, 1)
            blocks(7, rw32, range(C), range(2, 4)).then_inc(s_wturned, 1)
            pe.wait_ge(s_turned_out, 8)
            for c in range(C):
                last = product(halves(0)[:, c, :], [(wq0_t[:, a, chunk(c)], wk0_t[:, a, :]) for a in range(C)])
            last.then_inc(s_wturned, 1)
            for c in range(C):
                last = product(halves(1)[:, c, :], [(rwq1[:, a, chunk(c)], rwk1[:, a, :]) for a in range(C)])
            last.then_inc(s_wturned, 1)
            for c in range(C):
                last = product(small(2)[:, c, :], [(w2_t[:, a, chunk(c)], a_rep[:, a, :]) for a in range(C)])
            last.then_inc(s_wturned, 1)
            for c in range(C):
                product(bank[3][:, c:c + 1], [(rwk1[:, a, chunk(c)], bq_col[:, a:a + 1]) for a in range(C)])
                product(bank[3][:, 2 + c:3 + c], [(rwq1[:, a, chunk(c)], bk_col[:, a:a + 1]) for a in range(C)])
            product(bank[3][:, 4:5], [(bq_rep[:, a, :], bk_col[:, a:a + 1]) for a in range(C)]).then_inc(s_wturned, 1)
            product(bank[4][:, 0:D], [(beta_rep[:, k, :], w32_t[:, k, :]) for k in range(K)]).then_inc(s_wturned, 1)
            pe.wait_ge(s_turned_out, TURNS)
            pe.wait_ge(s_split_done, 1)

            def turn_pair(b, src):
                for c in range(C):
                    for g in range(PAIR):
                        last = turn(quarters(b)[:, c, g, :], src[:, g, chunk(c)])
                return last

            def mix(b, w, l):
                for m in range(C):
                    last = split_product(bank[b][:, m * 256:(m + 1) * 256],
                                         [((w[0][:, c, chunk(m)], w[1][:, c, chunk(m)]),
                                           (hT_hi[l][:, c, :, :], hT_lo[l][:, c, :, :])) for c in range(C)])
                return last

            def project(b, w, l):
                for g in range(PAIR):
                    last = split_product(halves(b)[:, g, :],
                                         [((hT_hi[l][:, c, g, :], hT_lo[l][:, c, g, :]),
                                           (w[0][:, c, :], w[1][:, c, :])) for c in range(C)])
                return last

            def scores(b, left, l):
                for g in range(PAIR):
                    last = product(small(b)[:, g, :], [(left[:, c, g, :], hT[l][:, c, g, :]) for c in range(C)])
                return last

            def step(t, live):
                if live(2):
                    pe.wait_ge(s_lo[2], upto(t - 1))
                    pe.wait_ge(s_final[0], upto(t))
                    split_product(bank[0][:, 0:256],
                                  [((wa_p[0][:, c, :], wa_p[1][:, c, :]),
                                    (hT_hi[2][:, c, :, :], hT_lo[2][:, c, :, :])) for c in range(C)]
                                  ).then_inc(s_sb_mm, 1)
                if live(1):
                    pe.wait_ge(s_xn[1], upto(t))
                    pe.wait_ge(s_agg_lo, upto(t - 3))
                    turn_pair(1, XN[1]).then_inc(s_turned[1], 1)
                if live(2):
                    project(2, w2_p, 2).then_inc(s_y_mm, 1)
                if live(1):
                    pe.wait_ge(s_lo[1], upto(t))
                    pe.wait_ge(s_tT_out, upto(t))
                    mix(5, m1_p, 1).then_inc(s_uT_mm, 1)
                if live(0):
                    pe.wait_ge(s_xn[0], upto(t + 1))
                    pe.wait_ge(s_PT_out, upto(t - 1))
                    pe.wait_ge(s_deg_out, upto(t - 3))
                    turn_pair(6, XN[0]).then_inc(s_turned[0], 1)
                if live(4):
                    pe.wait_ge(s_h1n_made, upto(t - 3))
                    for g in range(PAIR):
                        for k in range(K):
                            last = turn(bank[3 + g][:, k * P:(k + 1) * P], h1n[:, g, chunk(k)])
                    last.then_inc(s_h1T_mm, 1)
                if live(1):
                    pe.wait_ge(s_full[1], upto(t))
                    pe.wait_ge(s_soft_out, upto(t))
                    for g in range(PAIR):
                        last = product(bank[7][:, g:g + 1], [(hT[1][:, c, g, :], rvec[:, c:c + 1]) for c in range(C)])
                    last.then_inc(s_r1_mm, 1)
                    pe.wait_ge(s_uT_out, upto(t))
                    scores(1, uT, 1).then_inc(s_S1_mm, 1)
                if live(4):
                    pe.wait_ge(s_h1T_lo, upto(t - 3))
                    pe.wait_ge(s_tanh_made, upto(t - 1))
                    for g in range(PAIR):
                        last = split_product(halves(0)[:, g, :],
                                             [((h1T_hi[:, g, k, :], h1T_lo[:, g, k, :]),
                                               (w32_p[0][:, k, :], w32_p[1][:, k, :])) for k in range(K)])
                    last.then_inc(s_z_mm, 1)
                if live(2):
                    pe.wait_ge(s_a2_made, upto(t - 1))
                    pe.wait_ge(s_h1T_lo, upto(t - 3))
                    for g in range(PAIR):
                        last = turn(small(3)[:, g, :], a2m[:, g, :])
                    last.then_inc(s_AT_mm, 1)
                if live(1):
                    pe.wait_ge(s_y_out, upto(t - 1))
                    project(2, wv1_p, 1).then_inc(s_V1_mm, 1)
                if live(4):
                    pe.wait_ge(s_z_out, upto(t - 3))
                    for g in range(PAIR):
                        last = product(halves(0)[:, g, :], [(G[:, g, :], z[:, g, :])])
                    last.then_inc(s_Gz_mm, 1)
                if live(0):
                    pe.wait_ge(s_lo[0], upto(t + 1))
                    pe.wait_ge(s_uT_out, upto(t))
                    mix(5, m0_p, 0).then_inc(s_tT_mm, 1)
                if live(1):
                    pe.wait_ge(s_p1_made, upto(t))
                    pe.wait_ge(s_lo[0], upto(t + 1))
                    for g in range(PAIR):
                        last = turn(small(6)[:, g, :], p1[:, g, :])
                    last.then_inc(s_PT_mm, 1)
                if live(2):
                    pe.wait_ge(s_AT_out, upto(t - 1))
                    pe.wait_ge(s_h1T_lo, upto(t - 3))
                    for g in range(PAIR):
                        last = product(halves(4)[:, g, :], [(a2T[:, g, :], y2[:, g, :])])
                    last.then_inc(s_Ay_mm, 1)
                if live(0):
                    pe.wait_ge(s_full[0], upto(t + 1))
                    pe.wait_ge(s_tT_out, upto(t + 1))
                    pe.wait_ge(s_e1_made, upto(t))
                    scores(1, tT, 0).then_inc(s_S0_mm, 1)
                if live(3):
                    pe.wait_ge(s_a3_loaded, upto(t - 2, 16))
                    pe.wait_ge(s_AT_out, upto(t - 1))
                    for g in range(PAIR):
                        last = turn(small(3)[:, g, :], AD[3][:, g, :])
                    last.then_inc(s_AdT_mm, 1)
                if live(1):
                    pe.wait_ge(s_PT_out, upto(t))
                    pe.wait_ge(s_V1_out, upto(t))
                    for g in range(PAIR):
                        last = product(halves(2)[:, g, :], [(p1T[:, g, :], v1[:, g, :])])
                    last.then_inc(s_PV_mm, 1)
                if live(3):
                    pe.wait_ge(s_HT_made, upto(t - 2))
                    pe.wait_ge(s_PT_out, upto(t))
                    for g in range(PAIR):
                        last = product(bank[6][:, 256 + g:257 + g], [(HT[:, g, :], wcol[:, g:g + 1])])
                    last.then_inc(s_deg_mm, 1)
                    pe.wait_ge(s_bHT_made, upto(t - 2))
                    pe.wait_ge(s_final[2], upto(t - 1))
                    for g in range(PAIR):
                        last = product(small(4)[:, g, :], [(HT[:, g, :], bHT[:, g, :])])
                    last.then_inc(s_G_mm, 1)
                if live(0):
                    pe.wait_ge(s_w0_made, upto(t + 1))
                    pe.wait_ge(s_r1_out, upto(t))
                    product(bank[7][0:PAIR, 0:P], [(w0[:, :], ident[:, :])]).then_inc(s_wT_mm, 1)
                    pe.wait_ge(s_final[3], upto(t - 3))
                    project(0, wv0_p, 0).then_inc(s_V0_mm, 1)
                if live(3):
                    pe.wait_ge(s_G_out, upto(t - 2))
                    pe.wait_ge(s_h3_made, upto(t - 2))
                    pe.wait_ge(s_w0_made, upto(t + 1))
                    for g in range(PAIR):
                        for c in range(C):
                            last = product(quarters(1)[:, c, g, :], [(h3[:, g, chunk(c)], G[:, g, :])])
                    last.then_inc(s_agg_mm, 1)
                if live(0):
                    pe.wait_ge(s_prow_made, upto(t + 1))
                    product(bank[7][:, 0:PAIR], [(prow[:, :], ident[0:PAIR, 0:PAIR])]).then_inc(s_soft_mm, 1)
                if live(1):
                    pe.wait_ge(s_xn[2], upto(t))
                    pe.wait_ge(s_final[1], upto(t))
                    turn_pair(2, XN[2]).then_inc(s_turned[2], 1)
                if live(3):
                    pe.wait_ge(s_agg_lo, upto(t - 2))
                    pe.wait_ge(s_HT_made, upto(t - 2))
                    pe.wait_ge(s_G_out, upto(t - 2))
                    for g in range(PAIR):
                        last = split_product(bank[3 + g][:, :],
                                             [((aggT_hi[:, c, g, :], aggT_lo[:, c, g, :]),
                                               (w31_p[0][:, c, :], w31_p[1][:, c, :])) for c in range(C)])
                    last.then_inc(s_O1_mm, 1)

            steps(pe, step)


_INS = ["x", "adj", "nodemask", "L0_gnn_Wqk", "L0_gnn_Wv", "L1_gnn_Wq_w", "L1_gnn_Wq_b", "L1_gnn_Wk_w",
        "L1_gnn_Wk_b", "L1_gnn_Wv_w", "L1_gnn_Wv_b", "L2_gnn_w", "L2_gnn_a", "L3_gnn_W1", "L3_gnn_b1",
        "L3_gnn_gamma", "L3_gnn_beta", "L3_gnn_W2", "L3_gnn_b2"]


def kernel(**inputs):
    import numpy as np
    import concourse.bacc as bacc
    from concourse.bass_utils import run_bass_kernel_spmd as run

    nc = bacc.Bacc("TRN2", target_bir_lowering=False, num_devices=1)
    arrays, args = {}, []
    for name in _INS:
        a = np.ascontiguousarray(inputs[name])
        arrays[f"in_{name}_dram"] = a
        args.append(nc.dram_tensor(f"in_{name}_dram", a.shape, mybir.dt.from_np(a.dtype), kind="ExternalInput").ap())
    out = nc.dram_tensor("out_dram", arrays["in_x_dram"].shape, F32, kind="ExternalOutput").ap()
    build(nc, *args, out)
    return run(nc, [arrays], core_ids=[0]).results[0]["out_dram"]
```

```python
from contextlib import ExitStack

import concourse.bass as bass
from concourse import mybir

F32 = mybir.dt.float32
F32R = mybir.dt.float32r
ALU = mybir.AluOpType
ACT = mybir.ActivationFunctionType
AX_X = mybir.AxisListType.X

P = 128
PAIR = 2
EPS = 1e-5
TINY = 1.2e-38
LAST_OFF = 4


def build(nc, x, adj, mask, wqk0, wv0, wq1, bq1, wk1, bk1, wv1, bv1, w2, a2, w31, b31, gamma, beta,
          w32, b32, out):
    B, N, D = x.shape
    NG = B // PAIR
    C = D // P
    DH = w31.shape[0]
    K = DH // P
    assert N == P and C == 2 and K == 4
    INV = float(D) ** -0.5

    with ExitStack() as ctx:
        def sb(name, shape, dt=F32):
            return ctx.enter_context(nc.sbuf_tensor(name, shape, dt))

        def sem(name):
            return ctx.enter_context(nc.semaphore(name))

        bank = [ctx.enter_context(nc.psum_tensor(f"bank{i}", [P, 512], F32)) for i in range(8)]

        def quarters(b):
            return bank[b][:, :].rearrange("p (c b n) -> p c b n", c=2, b=2)

        def halves(b):
            return bank[b][:, :].rearrange("p (b d) -> p b d", b=2)

        def small(b):
            return bank[b][:, 0:256].rearrange("p (b d) -> p b d", b=2)

        ident = sb("ident", [P, P])
        rwqk0, rwv0 = sb("rwqk0", [P, C, 2 * D]), sb("rwv0", [P, C, D])
        rwq1, rwk1, rwv1 = sb("rwq1", [P, C, D]), sb("rwk1", [P, C, D]), sb("rwv1", [P, C, D])
        rw2, rw31, rw32 = sb("rw2", [P, C, D]), sb("rw31", [P, K, D]), sb("rw32", [P, C, DH])
        bq_col, bk_col, a_col = sb("bq_col", [P, C]), sb("bk_col", [P, C]), sb("a_col", [P, C])
        gamma_col, beta_col = sb("gamma_col", [P, K]), sb("beta_col", [P, K])
        bv_bc, b1_bc, b2_bc = sb("bv_bc", [P, D]), sb("b1_bc", [P, DH]), sb("b2_bc", [P, D])
        ones = sb("ones", [P, P])
        a_rep, beta_rep = sb("a_rep", [P, C, P]), sb("beta_rep", [P, K, P])
        bq_rep = sb("bq_rep", [P, C, P])
        wq0_t, wk0_t, w2_t = (sb(n, [P, C, D]) for n in ("wq0_t", "wk0_t", "w2_t"))
        DV = D + 2
        wv1_t = sb("wv1_t", [P, C, DV])
        w31_t, w32_t, w32_g = sb("w31_t", [P, C, DH]), sb("w32_t", [P, K, D]), sb("w32_g", [P, K, D])
        m0, m1 = sb("m0", [P, C, D]), sb("m1", [P, C, D])
        wa = sb("wa", [P, C, P])
        vecs = sb("vecs", [P, 5])
        bw2 = sb("bw2", [P, D])
        ubias, rconst = vecs[:, 0:2], vecs[:, 4:5]

        def parts(name, shape):
            return sb(name + "_hi", shape, F32R), sb(name + "_lo", shape, F32R)

        m0_p, m1_p, wv0_p, w2_p = (parts(n, [P, C, D]) for n in ("pm0", "pm1", "pwv0", "pw2"))
        wv1_p = parts("pwv1", [P, C, DV])
        wa_p = parts("pwa", [P, C, P])
        w31_p, w32_p = parts("pw31", [P, C, DH]), parts("pw32", [P, K, D])

        x_in = sb("x_in", [P, PAIR, D])
        X = [sb(f"X{l}", [P, PAIR, D]) for l in range(4)]
        x_out = sb("x_out", [P, PAIR, D])
        H = [sb(f"H{l}", [P, PAIR, D]) for l in range(4)]
        stats = [sb(f"stats{l}", [P, PAIR, 6]) for l in range(5)]
        mv = [sb(f"mv{l}", [P, PAIR, 2]) for l in range(5)]
        vare = [sb(f"vare{l}", [P, PAIR, 1]) for l in range(5)]
        rstd = [sb(f"rstd{l}", [P, PAIR, 1]) for l in range(5)]
        nmean = [sb(f"nmean{l}", [P, PAIR, 1]) for l in range(5)]
        nmr = [sb(f"nmr{l}", [P, PAIR, 1]) for l in range(5)]
        eps_t, half_t, neg_t = sb("eps_t", [P, PAIR, 1]), sb("half_t", [P, PAIR, 1]), sb("neg_t", [P, PAIR, 1])
        dve_scratch = sb("dve_scratch", [P, 5])
        hT_hi = [sb(f"hT{l}_hi", [P, C, PAIR, P], F32R) for l in range(3)]
        hT_lo = [sb(f"hT{l}_lo", [P, C, PAIR, P], F32R) for l in range(3)]
        hT = [sb(f"hT{l}", [P, C, PAIR, P]) for l in range(2)]
        AD = [sb(f"AD{l}", [P, PAIR, P]) for l in range(4)]
        mask_bc = sb("mask_bc", [P, PAIR, P])
        mask_rows = sb("mask_rows", [PAIR, P])
        adm = sb("adm", [P, PAIR, P])
        tT, uT = sb("tT", [P, C, PAIR, P]), sb("uT", [P, C, PAIR, P])
        junk, junk0 = sb("junk", [P, PAIR, P]), sb("junk0", [P, PAIR, P])
        w0 = sb("w0", [P, PAIR])
        wrow, erow, prow = (sb(n, [PAIR, P]) for n in ("wrow", "erow", "prow"))
        nmax, esum, einv = (sb(n, [PAIR, 1]) for n in ("nmax", "esum", "einv"))
        soft = sb("soft", [P, PAIR])
        r1 = sb("r1", [P, PAIR])
        e1, p1, p1T = sb("e1", [P, PAIR, P]), sb("p1", [P, PAIR, P]), sb("p1T", [P, PAIR, P])
        v1, xv1 = sb("v1", [P, PAIR, D]), sb("xv1", [P, PAIR, D])
        sum1, inv1 = sb("sum1", [P, PAIR]), sb("inv1", [P, PAIR])
        s2 = sb("s2", [P, PAIR])
        th2, lr2, e2 = (sb(n, [P, PAIR, P]) for n in ("th2", "lr2", "e2"))
        a2m, a2T = sb("a2m", [P, PAIR, P]), sb("a2T", [P, PAIR, P])
        sum2, inv2, asum2, ratio2 = (sb(n, [P, PAIR]) for n in ("sum2", "inv2", "asum2", "ratio2"))
        y2 = sb("y2", [P, PAIR, D])
        HT, bHT, G = sb("HT", [P, PAIR, P]), sb("bHT", [P, PAIR, P]), sb("G", [P, PAIR, P])
        wcol = sb("wcol", [P, PAIR])
        cnt, cnt1, binv = (sb(n, [P, PAIR]) for n in ("cnt", "cnt1", "binv"))
        deg, deg1, dinv, Dn = (sb(n, [P, PAIR]) for n in ("deg", "deg1", "dinv", "Dn"))
        aggT_hi, aggT_lo = parts("aggT", [P, C, PAIR, P])
        o1, r3, h1n = (sb(n, [P, PAIR, DH]) for n in ("o1", "r3", "h1n"))
        h1T_hi, h1T_lo = parts("h1T", [P, PAIR, K, P])
        z = sb("z", [P, PAIR, D])
        xb3a, xb3 = sb("xb3a", [P, PAIR, D]), sb("xb3", [P, PAIR, D])

        s_w_loaded = sem("s_w_loaded")
        s_b_loaded = sem("s_b_loaded")
        s_ident_made = sem("s_ident_made")
        s_reps_made = sem("s_reps_made")
        s_consts = sem("s_consts")
        s_wturned = sem("s_wturned")
        s_turned_out = sem("s_turned_out")
        s_hi_done = sem("s_hi_done")
        s_split_done = sem("s_split_done")
        s_x_loaded = sem("s_x_loaded")
        s_x_stored = sem("s_x_stored")
        s_mbc_loaded = sem("s_mbc_loaded")
        s_mrow_loaded = sem("s_mrow_loaded")
        s_a0_loaded = sem("s_a0_loaded")
        s_a1_loaded = sem("s_a1_loaded")
        s_a2_loaded = sem("s_a2_loaded")
        s_a3_loaded = sem("s_a3_loaded")
        s_x0_copied = sem("s_x0_copied")
        s_adm_made = sem("s_adm_made")
        s_tT_mm = sem("s_tT_mm")
        s_tT_out = sem("s_tT_out")
        s_S0_mm = sem("s_S0_mm")
        s_w0_made = sem("s_w0_made")
        s_wT_mm = sem("s_wT_mm")
        s_wrow_made = sem("s_wrow_made")
        s_nmax_made = sem("s_nmax_made")
        s_erow_made = sem("s_erow_made")
        s_einv_made = sem("s_einv_made")
        s_prow_made = sem("s_prow_made")
        s_soft_mm = sem("s_soft_mm")
        s_soft_out = sem("s_soft_out")
        s_V0_mm = sem("s_V0_mm")
        s_uT_mm = sem("s_uT_mm")
        s_uT_out = sem("s_uT_out")
        s_r1_out = sem("s_r1_out")
        s_S1_mm = sem("s_S1_mm")
        s_e1_made = sem("s_e1_made")
        s_p1_made = sem("s_p1_made")
        s_inv1_made = sem("s_inv1_made")
        s_PT_mm = sem("s_PT_mm")
        s_PT_out = sem("s_PT_out")
        s_V1_mm = sem("s_V1_mm")
        s_V1_out = sem("s_V1_out")
        s_PV_mm = sem("s_PV_mm")
        s_xv1_made = sem("s_xv1_made")
        s_sb_mm = sem("s_sb_mm")
        s_s2_made = sem("s_s2_made")
        s_tanh_made = sem("s_tanh_made")
        s_lr_made = sem("s_lr_made")
        s_e2_made = sem("s_e2_made")
        s_a2_made = sem("s_a2_made")
        s_inv2_made = sem("s_inv2_made")
        s_asum_made = sem("s_asum_made")
        s_ratio_made = sem("s_ratio_made")
        s_AT_mm = sem("s_AT_mm")
        s_AT_out = sem("s_AT_out")
        s_y_mm = sem("s_y_mm")
        s_y_out = sem("s_y_out")
        s_Ay_mm = sem("s_Ay_mm")
        s_AdT_mm = sem("s_AdT_mm")
        s_HT_made = sem("s_HT_made")
        s_cnt1_made = sem("s_cnt1_made")
        s_binv_made = sem("s_binv_made")
        s_bHT_made = sem("s_bHT_made")
        s_wcol_made = sem("s_wcol_made")
        s_deg_mm = sem("s_deg_mm")
        s_deg_out = sem("s_deg_out")
        s_deg1_made = sem("s_deg1_made")
        s_dinv_made = sem("s_dinv_made")
        s_Dn_made = sem("s_Dn_made")
        s_G_mm = sem("s_G_mm")
        s_G_out = sem("s_G_out")
        s_agg_mm = sem("s_agg_mm")
        s_agg_hi = sem("s_agg_hi")
        s_agg_lo = sem("s_agg_lo")
        s_O1_mm = [sem(f"s_O1_mm{g}") for g in range(PAIR)]
        s_o1_made = [sem(f"s_o1_made{g}") for g in range(PAIR)]
        s_r3_made = [sem(f"s_r3_made{g}") for g in range(PAIR)]
        s_h1n_made = sem("s_h1n_made")
        s_h1T_mm = [sem(f"s_h1T_mm{g}") for g in range(PAIR)]
        s_h1T_hi = [sem(f"s_h1T_hi{g}") for g in range(PAIR)]
        s_h1T_lo = [sem(f"s_h1T_lo{g}") for g in range(PAIR)]
        s_z_mm = sem("s_z_mm")
        s_z_out = sem("s_z_out")
        s_Gz_mm = sem("s_Gz_mm")
        s_xb3a_made = sem("s_xb3a_made")
        s_xb3_made = sem("s_xb3_made")
        s_stats = [sem(f"s_stats{l}") for l in range(5)]
        s_mv = [sem(f"s_mv{l}") for l in range(5)]
        s_vare = [sem(f"s_vare{l}") for l in range(5)]
        s_rstd = [sem(f"s_rstd{l}") for l in range(5)]
        s_terms = [sem(f"s_terms{l}") for l in range(4)]
        s_nmean = [sem(f"s_nmean{l}") for l in range(4)]
        s_h = [sem(f"s_h{l}") for l in range(4)]
        s_turned = [sem(f"s_turned{l}") for l in range(3)]
        s_hi = [sem(f"s_hi{l}") for l in range(3)]
        s_lo = [sem(f"s_lo{l}") for l in range(3)]
        s_full = [sem(f"s_full{l}") for l in range(2)]
        s_final = [sem(f"s_final{l}") for l in range(4)]

        def upto(n, unit=1):
            return (min(max(n, 0), NG) if isinstance(n, int) else n) * unit

        turn_jobs = [(wq0_t[:, :, :], 512), (wk0_t[:, :, :], 512), (wv1_t[:, :, 0:D], 512), (w2_t[:, :, :], 512),
                     (w31_t[:, 0, :], 512), (w31_t[:, 1, :], 512), (0, "gamma"), (2, "gamma"),
                     (m0[:, :, :], 512), (m1[:, :, :], 512), (wa[:, :, :], 256), (vecs[:, :], "vecs"), (bw2[:, :], 256)]
        TURNS = len(turn_jobs)
        splits = [(m0, m0_p), (m1, m1_p), (rwv0, wv0_p), (wv1_t, wv1_p), (rw2, w2_p), (wa, wa_p),
                  (w31_t, w31_p), (w32_g, w32_p)]
        VBANK = [2, 7]
        TBANK = [6, 1, 2]

        FIRST, LAST = LAST_OFF + 1, NG - 2

        def steps(eng, step):
            for t in range(-1, FIRST):
                step(t, lambda off, t=t: 0 <= t - off < NG)
            with eng.Fori(FIRST, LAST + 1) as t:
                step(t, lambda off: True)
            for t in range(LAST + 1, NG + LAST_OFF):
                step(t, lambda off, t=t: 0 <= t - off < NG)

        block = ctx.enter_context(nc.Block())

        def col(v):
            return v.rearrange("(c p) -> p c", p=P)

        @block.sync
        def _(sp):
            big = [(rwqk0, wqk0), (rwv0, wv0), (rwq1, wq1), (rwk1, wk1), (rwv1, wv1), (rw2, w2),
                   (rw31, w31), (rw32, w32)]
            for dst, src in big:
                sp.dma_start(dst[:, :, :], src.rearrange("(c p) n -> p c n", p=P)).then_inc(s_w_loaded, 16)

            def rows(v, g):
                return v[bass.ds(g * PAIR, PAIR)] if not isinstance(g, int) else v[g * PAIR:(g + 1) * PAIR]

            def load(dst, src, g, signal, free, n):
                sp.wait_ge(free, upto(n))
                sp.dma_start(dst[:, :, :], rows(src, g).rearrange("b p d -> p b d")).then_inc(signal, 16)

            def step(t, live):
                if live(-1):
                    if isinstance(t, int) and t == -1:
                        load(x_in, x, 0, s_x_loaded, s_x0_copied, 0)
                if live(0):
                    load(AD[0], adj, t, s_a0_loaded, s_adm_made, t)
                    sp.wait_ge(s_adm_made, upto(t))
                    g = t
                    mrows = rows(mask, g)
                    sp.dma_start(mask_bc[:, :, :], mrows.unsqueeze(0).broadcast_to([P, PAIR, P])
                                 ).then_inc(s_mbc_loaded, 16)
                    sp.wait_ge(s_wrow_made, upto(t))
                    sp.dma_start(mask_rows[:, :], mrows).then_inc(s_mrow_loaded, 16)
                if live(1):
                    load(AD[1], adj, t - 1, s_a1_loaded, s_p1_made, t - 1)
                if live(2):
                    load(AD[2], adj, t - 2, s_a2_loaded, s_a2_made, t - 2)
                if live(3):
                    load(AD[3], adj, t - 3, s_a3_loaded, s_AdT_mm, t - 3)
                if live(0) and live(-1):
                    load(x_in, x, t + 1, s_x_loaded, s_x0_copied, t + 1)

            steps(sp, step)

        @block.gpsimd
        def _(pool):
            gp = nc.gpsimd
            gp.memset(ident[:, :], 0.0).then_inc(s_consts, 1)
            gp.memset(ones[:, :], 1.0)
            gp.memset(eps_t[:, :, :], EPS)
            gp.memset(wv1_t[:, :, D + 1], 0.0)
            gp.memset(half_t[:, :, :], -0.5)
            gp.memset(neg_t[:, :, :], -1.0).then_inc(s_consts, 1)
            pool.wait_ge(s_consts, 2)
            gp.affine_select(out=ident[:, :], in_=ident[:, :], compare_op=ALU.not_equal, fill=1.0,
                             base=0, pattern=[[-1, P]], channel_multiplier=1).then_inc(s_ident_made, 1)
            pool.wait_ge(s_b_loaded, 16 * 8)
            for c in range(C):
                gp.tensor_scalar(a_rep[:, c, :], ones[:, :], a_col[:, c:c + 1], None, ALU.mult)
                gp.tensor_scalar(bq_rep[:, c, :], ones[:, :], bq_col[:, c:c + 1], None, ALU.mult)
            for k in range(K):
                last = gp.tensor_scalar(beta_rep[:, k, :], ones[:, :], beta_col[:, k:k + 1], None, ALU.mult)
            last.then_inc(s_reps_made, 1)

            def rstd_of(l, n, used):
                pool.wait_ge(s_mv[l], upto(n))
                pool.wait_ge(used, upto(n - 1))
                gp.tensor_tensor(vare[l][:, :, :], mv[l][:, :, 1:2], eps_t[:, :, :], ALU.add
                                 ).then_inc(s_vare[l], 1)
                pool.wait_ge(s_vare[l], upto(n))
                gp.tensor_tensor(rstd[l][:, :, :], vare[l][:, :, :], half_t[:, :, :], ALU.pow
                                 ).then_inc(s_rstd[l], 1)

            def norm_terms(l, n, used):
                rstd_of(l, n, used)
                gp.tensor_tensor(nmean[l][:, :, :], mv[l][:, :, 0:1], neg_t[:, :, :], ALU.mult).then_inc(s_nmean[l], 1)
                pool.wait_ge(s_nmean[l], upto(n))
                pool.wait_ge(s_rstd[l], upto(n))
                gp.tensor_tensor(nmr[l][:, :, :], nmean[l][:, :, :], rstd[l][:, :, :], ALU.mult
                                 ).then_inc(s_terms[l], 1)

            def bc(v):
                return v[:, :].unsqueeze(1).broadcast_to([P, PAIR, D])

            def step(t, live):
                if live(1):
                    pool.wait_ge(s_lo[1], upto(t))
                    pool.wait_ge(s_S1_mm, upto(t - 1))
                    gp.tensor_tensor(hT[1][:, :, :, :], hT_hi[1][:, :, :, :].bitcast(F32),
                                     hT_lo[1][:, :, :, :].bitcast(F32), ALU.add).then_inc(s_full[1], 1)
                if live(4):
                    rstd_of(4, t - 3, s_h1n_made)
                if live(3):
                    pool.wait_ge(s_final[2], upto(t - 2))
                    gp.tensor_tensor(xb3a[:, :, :], X[3][:, :, :], bc(b2_bc), ALU.add).then_inc(s_xb3a_made, 1)
                if live(0):
                    pool.wait_ge(s_a0_loaded, upto(t + 1, 16))
                    pool.wait_ge(s_mbc_loaded, upto(t + 1, 16))
                    pool.wait_ge(s_w0_made, upto(t))
                    gp.tensor_tensor(adm[:, :, :], AD[0][:, :, :], mask_bc[:, :, :], ALU.mult
                                     ).then_inc(s_adm_made, 1)
                if live(3):
                    norm_terms(3, t - 2, s_h[3])
                if live(1):
                    pool.wait_ge(s_final[0], upto(t))
                    pool.wait_ge(s_final[1], upto(t - 1))
                    gp.tensor_tensor(xv1[:, :, :], X[1][:, :, :], bc(bv_bc), ALU.add).then_inc(s_xv1_made, 1)
                if live(-1):
                    norm_terms(0, t + 2, s_h[0])
                if live(0):
                    norm_terms(1, t + 1, s_h[1])
                if live(1):
                    norm_terms(2, t, s_h[2])
                if live(-1):
                    pool.wait_ge(s_full[0], upto(t + 2))
                    pool.wait_ge(s_V0_mm, upto(t + 1))
                    gp.tensor_tensor(hT_lo[0][:, :, :, :], hT[0][:, :, :, :], hT_hi[0][:, :, :, :].bitcast(F32),
                                     ALU.subtract).then_inc(s_lo[0], 1)
                if live(3):
                    pool.wait_ge(s_xb3a_made, upto(t - 2))
                    pool.wait_ge(s_h[3], upto(t - 2))
                    pool.wait_ge(s_final[3], upto(t - 3))
                    gp.tensor_tensor(xb3[:, :, :], xb3a[:, :, :], H[3][:, :, :], ALU.add).then_inc(s_xb3_made, 1)

            steps(pool, step)

        @block.scalar
        def _(act):
            sc = nc.scalar
            vec = [(bq_col, col(bq1)), (bk_col, col(bk1)), (a_col, col(a2)), (gamma_col, col(gamma)),
                   (beta_col, col(beta)), (bv_bc, bv1.unsqueeze(0).broadcast_to([P, D])),
                   (b1_bc, b31.unsqueeze(0).broadcast_to([P, DH])), (b2_bc, b32.unsqueeze(0).broadcast_to([P, D]))]
            for dst, src in vec:
                act.dma_start(dst[:, :], src, allow_slow_non_contiguous=True).then_inc(s_b_loaded, 16)
            act.wait_ge(s_w_loaded, 16 * 8)
            act.wait_ge(s_turned_out, TURNS)
            for whole, (hi, lo) in splits:
                last = sc.activation(hi[:, :, :], whole[:, :, :], ACT.Copy)
            last.then_inc(s_hi_done, 1)

            def store(g):
                dst = out[g * PAIR:(g + 1) * PAIR] if isinstance(g, int) else out[bass.ds(g * PAIR, PAIR)]
                act.dma_start(dst.rearrange("b p d -> p b d"), x_out[:, :, :]).then_inc(s_x_stored, 16)

            def normalise(l, n, src, used):
                act.wait_ge(s_terms[l], upto(n))
                act.wait_ge(used, upto(n - 1))
                for b in range(PAIR):
                    last = sc.activation(H[l][:, b, :], src[:, b, :], ACT.Relu,
                                         bias=nmr[l][:, b, 0:1], scale=rstd[l][:, b, 0:1])
                last.then_inc(s_h[l], 1)

            def high(l, n):
                act.wait_ge(s_turned[l], upto(n))
                act.wait_ge((s_V0_mm, s_V1_mm, s_y_mm)[l], upto(n - 1))
                act.wait_ge((s_lo[0], s_full[1], s_lo[2])[l], upto(n - 1))
                sc.activation(hT_hi[l][:, :, :, :], quarters(TBANK[l]), ACT.Copy).then_inc(s_hi[l], 1)

            def hidden_relu(b, n):
                act.wait_ge(s_o1_made[b], upto(n))
                act.wait_ge(s_h1n_made, upto(n - 1))
                sc.activation(r3[:, b, :], o1[:, b, :], ACT.Relu).then_inc(s_r3_made[b], 1)

            def step(t, live):
                if live(1):
                    high(1, t)
                if live(4):
                    hidden_relu(1, t - 3)
                if live(2):
                    high(2, t - 1)
                if live(0):
                    act.wait_ge(s_tT_mm, upto(t + 1))
                    act.wait_ge(s_S0_mm, upto(t))
                    sc.activation(tT[:, :, :, :], quarters(0), ACT.Copy).then_inc(s_tT_out, 1)
                if live(1):
                    act.wait_ge(s_uT_mm, upto(t))
                    act.wait_ge(s_S1_mm, upto(t - 1))
                    for m in range(C):
                        last = sc.activation(uT[:, m, :, :], quarters(5)[:, m, :, :], ACT.Identity,
                                             bias=ubias[:, m:m + 1])
                    last.then_inc(s_uT_out, 1)
                if live(2):
                    act.wait_ge(s_s2_made, upto(t - 1))
                    act.wait_ge(s_lr_made, upto(t - 2))
                    for b in range(PAIR):
                        last = sc.activation(th2[:, b, :], small(0)[:, b, :], ACT.Tanh,
                                             bias=s2[:, b:b + 1], scale=0.125)
                    last.then_inc(s_tanh_made, 1)
                if live(1):
                    act.wait_ge(s_V1_mm, upto(t))
                    act.wait_ge(s_PV_mm, upto(t - 1))
                    for b in range(PAIR):
                        last = sc.activation(v1[:, b, :], bank[VBANK[b]][:, 0:D], ACT.Copy)
                    last.then_inc(s_V1_out, 1)
                if live(2):
                    act.wait_ge(s_lr_made, upto(t - 1))
                    act.wait_ge(s_a2_made, upto(t - 2))
                    sc.activation(e2[:, :, :], lr2[:, :, :], ACT.Exp, scale=8.0).then_inc(s_e2_made, 1)
                if live(2):
                    act.wait_ge(s_y_mm, upto(t - 1))
                    act.wait_ge(s_Ay_mm, upto(t - 2))
                    sc.activation(y2[:, :, :], halves(6), ACT.Copy).then_inc(s_y_out, 1)
                if live(1):
                    act.wait_ge(s_S1_mm, upto(t))
                    act.wait_ge(s_r1_out, upto(t))
                    act.wait_ge(s_p1_made, upto(t - 1))
                    for b in range(PAIR):
                        last = sc.activation(e1[:, b, :], small(1)[:, b, :], ACT.Exp, bias=r1[:, b:b + 1])
                    last.then_inc(s_e1_made, 1)
                if live(4):
                    act.wait_ge(s_z_mm, upto(t - 4))
                    act.wait_ge(s_h1T_lo[1], upto(t - 4))
                    for b in range(PAIR):
                        act.wait_ge(s_h1T_mm[b], upto(t - 3))
                        sc.activation(h1T_hi[:, b, :, :], bank[3 + b][:, :].rearrange("p (k n) -> p k n", k=K),
                                      ACT.Copy).then_inc(s_h1T_hi[b], 1)
                if live(3):
                    act.wait_ge(s_xb3_made, upto(t - 3))
                    normalise(3, t - 2, X[3], s_agg_mm)
                if live(1):
                    act.wait_ge(s_PT_mm, upto(t))
                    act.wait_ge(s_AT_mm, upto(t - 1))
                    act.wait_ge(s_PV_mm, upto(t - 1))
                    sc.activation(p1T[:, :, :], small(6), ACT.Copy).then_inc(s_PT_out, 1)
                if live(2):
                    act.wait_ge(s_AT_mm, upto(t - 1))
                    act.wait_ge(s_Ay_mm, upto(t - 2))
                    sc.activation(a2T[:, :, :], bank[6][:, 256:512].rearrange("p (b n) -> p b n", b=PAIR), ACT.Copy
                                  ).then_inc(s_AT_out, 1)
                if live(0):
                    act.wait_ge(s_nmax_made, upto(t + 1))
                    act.wait_ge(s_prow_made, upto(t))
                    sc.activation(erow[:, :], wrow[:, :], ACT.Exp, bias=nmax[:, :], accum_out=esum[:, :]
                                  ).then_inc(s_erow_made, 1)
                if live(-1):
                    normalise(0, t + 2, x_in, s_turned[0])
                if live(3):
                    act.wait_ge(s_binv_made, upto(t - 2))
                    act.wait_ge(s_G_mm, upto(t - 3))
                    for b in range(PAIR):
                        last = sc.activation(bHT[:, b, :], HT[:, b, :], ACT.Copy, scale=binv[:, b:b + 1])
                    last.then_inc(s_bHT_made, 1)
                if live(3):
                    act.wait_ge(s_G_mm, upto(t - 2))
                    act.wait_ge(s_Gz_mm, upto(t - 3))
                    sc.activation(G[:, :, :], small(4), ACT.Copy).then_inc(s_G_out, 1)
                if live(-1):
                    act.wait_ge(s_final[0], upto(t + 1))
                    sc.activation(X[0][:, :, :], x_in[:, :, :], ACT.Copy).then_inc(s_x0_copied, 1)
                if live(0):
                    normalise(1, t + 1, X[1], s_turned[1])
                if live(3):
                    act.wait_ge(s_agg_mm, upto(t - 2))
                    act.wait_ge(s_O1_mm[1], upto(t - 3))
                    act.wait_ge(s_agg_lo, upto(t - 3))
                    sc.activation(aggT_hi[:, :, :, :], quarters(1), ACT.Copy).then_inc(s_agg_hi, 1)
                if live(-1):
                    high(0, t + 2)
                    act.wait_ge(s_S0_mm, upto(t + 1))
                    sc.activation(hT[0][:, :, :, :], quarters(6), ACT.Copy).then_inc(s_full[0], 1)
                if live(4):
                    act.wait_ge(s_final[3], upto(t - 3))
                    store(t - 4)
                if live(1):
                    normalise(2, t, X[2], s_turned[2])
                if live(3):
                    hidden_relu(0, t - 2)

            steps(act, step)
            act.wait_ge(s_x_stored, 16 * NG)

        @block.vector
        def _(dve):
            v = nc.vector
            for j in range(len(turn_jobs)):
                dve.wait_ge(s_wturned, j + 1)
                dst, kind = turn_jobs[j]
                src = bank[j % 8]
                if kind == "gamma":
                    dve.wait_ge(s_b_loaded, 16 * 8)
                    k0 = dst
                    v.tensor_copy(w32_t[:, k0:k0 + 2, :], halves(j % 8))
                    for k in range(2):
                        last = v.tensor_scalar(w32_g[:, k0 + k, :], halves(j % 8)[:, k, :],
                                               gamma_col[:, k0 + k:k0 + k + 1], None, ALU.mult)
                    last.then_inc(s_turned_out, 1)
                elif kind == "vecs":
                    v.tensor_copy(dst, src[:, 0:5])
                    v.tensor_copy(wv1_t[:, :, D], src[:, 2:4]).then_inc(s_turned_out, 1)
                else:
                    v.tensor_copy(dst, src[:, 0:kind]).then_inc(s_turned_out, 1)
            dve.wait_ge(s_hi_done, 1)
            for whole, (hi, lo) in splits:
                last = v.tensor_tensor(lo[:, :, :], whole[:, :, :], hi[:, :, :].bitcast(F32), ALU.subtract)
            last.then_inc(s_split_done, 1)

            def stats_of(l, n, src):
                dve.wait_ge(s_mv[l], upto(n - 1))
                for b in range(PAIR):
                    last = v.bn_stats(stats[l][:, b, :], src[:, b, :])
                last.then_inc(s_stats[l], 1)

            def aggregate(l, n):
                dve.wait_ge(s_stats[l], upto(n))
                dve.wait_ge(s_terms[l] if l < 4 else s_h1n_made, upto(n - 1))
                v.memset(dve_scratch[:, l:l + 1], 0.0)
                for b in range(PAIR):
                    last = v.bn_aggr(mv[l][:, b, :], stats[l][:, b, :])
                last.then_inc(s_mv[l], 1)

            def low(l, n):
                dve.wait_ge(s_hi[l], upto(n))
                v.tensor_tensor(hT_lo[l][:, :, :, :].rearrange("p c b n -> p (c b n)"), bank[TBANK[l]][:, :],
                                       hT_hi[l][:, :, :, :].bitcast(F32).rearrange("p c b n -> p (c b n)"),
                                ALU.subtract).then_inc(s_lo[l], 1)

            def weighted_sum(dst, prod, acc, scale):
                for b in range(PAIR):
                    last = v.tensor_tensor_reduce(out=dst[:, b, :], in0=prod[0][:, b, :], in1=prod[1][:, b, :],
                                                  scale=scale, scalar=0.0, op0=ALU.mult, op1=ALU.add,
                                                  accum_out=acc[:, b:b + 1])
                return last

            def step(t, live):
                if live(1):
                    low(1, t)
                if live(2):
                    low(2, t - 1)
                if live(4):
                    dve.wait_ge(s_mv[4], upto(t - 4))
                    for b in range(PAIR):
                        dve.wait_ge(s_r3_made[b], upto(t - 3))
                        last = v.bn_stats(stats[4][:, b, :], r3[:, b, :])
                    last.then_inc(s_stats[4], 1)
                if live(4):
                    aggregate(4, t - 3)
                if live(3):
                    dve.wait_ge(s_final[2], upto(t - 2))
                    stats_of(3, t - 2, X[3])
                if live(2):
                    dve.wait_ge(s_a2_loaded, upto(t - 1, 16))
                    dve.wait_ge(s_ratio_made, upto(t - 2))
                    v.tensor_reduce(asum2[:, :], AD[2][:, :, :], AX_X, ALU.add).then_inc(s_asum_made, 1)
                if live(2):
                    dve.wait_ge(s_sb_mm, upto(t - 1))
                    dve.wait_ge(s_tanh_made, upto(t - 2))
                    dve.wait_ge(s_s2_made, upto(t - 2))
                    for b in range(PAIR):
                        last = v.tensor_tensor_reduce(out=junk[:, b, :], in0=small(0)[:, b, :], in1=ident[:, :],
                                                      scale=0.125, scalar=0.0, op0=ALU.mult, op1=ALU.add,
                                                      accum_out=s2[:, b:b + 1])
                    last.then_inc(s_s2_made, 1)
                if live(4):
                    dve.wait_ge(s_rstd[4], upto(t - 3))
                    dve.wait_ge(s_h1T_mm[1], upto(t - 4))
                    for b in range(PAIR):
                        last = v.tensor_scalar(h1n[:, b, :], r3[:, b, :], mv[4][:, b, 0:1], rstd[4][:, b, 0:1],
                                               ALU.subtract, ALU.mult)
                    last.then_inc(s_h1n_made, 1)
                if live(2):
                    dve.wait_ge(s_tanh_made, upto(t - 1))
                    dve.wait_ge(s_e2_made, upto(t - 2))
                    v.scalar_tensor_tensor(lr2[:, :, :], th2[:, :, :], 0.1, th2[:, :, :], ALU.mult, ALU.max
                                           ).then_inc(s_lr_made, 1)
                if live(3):
                    aggregate(3, t - 2)
                if live(1):
                    dve.wait_ge(s_V1_out, upto(t))
                    dve.wait_ge(s_e1_made, upto(t - 1))
                    for b in range(PAIR):
                        last = v.tensor_scalar(r1[:, b:b + 1], bank[VBANK[b]][:, D:D + 1], rconst, None, ALU.add)
                    last.then_inc(s_r1_out, 1)
                if live(2):
                    dve.wait_ge(s_e2_made, upto(t - 1))
                    dve.wait_ge(s_AT_mm, upto(t - 2))
                    dve.wait_ge(s_inv2_made, upto(t - 2))
                    weighted_sum(a2m, (e2, AD[2]), sum2, 1.0).then_inc(s_a2_made, 1)
                if live(2):
                    dve.wait_ge(s_a2_made, upto(t - 1))
                    dve.wait_ge(s_ratio_made, upto(t - 2))
                    v.reciprocal(inv2[:, :], sum2[:, :]).then_inc(s_inv2_made, 1)
                if live(2):
                    dve.wait_ge(s_inv2_made, upto(t - 1))
                    dve.wait_ge(s_final[2], upto(t - 2))
                    v.tensor_tensor(ratio2[:, :], inv2[:, :], asum2[:, :], ALU.mult).then_inc(s_ratio_made, 1)
                if live(1):
                    dve.wait_ge(s_e1_made, upto(t))
                    dve.wait_ge(s_a1_loaded, upto(t, 16))
                    dve.wait_ge(s_PT_mm, upto(t - 1))
                    dve.wait_ge(s_inv1_made, upto(t - 1))
                    weighted_sum(p1, (e1, AD[1]), sum1, 1.0).then_inc(s_p1_made, 1)
                if live(1):
                    dve.wait_ge(s_p1_made, upto(t))
                    dve.wait_ge(s_final[1], upto(t - 1))
                    v.reciprocal(inv1[:, :], sum1[:, :]).then_inc(s_inv1_made, 1)
                if live(4):
                    dve.wait_ge(s_z_mm, upto(t - 4))
                    for b in range(PAIR):
                        dve.wait_ge(s_h1T_hi[b], upto(t - 3))
                        v.tensor_tensor(h1T_lo[:, b, :, :], bank[3 + b][:, :].rearrange(
                            "p (k n) -> p k n", k=K), h1T_hi[:, b, :, :].bitcast(F32), ALU.subtract
                        ).then_inc(s_h1T_lo[b], 1)
                if live(0):
                    dve.wait_ge(s_S0_mm, upto(t + 1))
                    dve.wait_ge(s_adm_made, upto(t + 1))
                    dve.wait_ge(s_wT_mm, upto(t))
                    dve.wait_ge(s_w0_made, upto(t))
                    weighted_sum(junk0, (small(1), adm), w0, INV).then_inc(s_w0_made, 1)
                if live(-1):
                    dve.wait_ge(s_x_loaded, upto(t + 2, 16))
                    stats_of(0, t + 2, x_in)
                    aggregate(0, t + 2)
                if live(0):
                    dve.wait_ge(s_wT_mm, upto(t + 1))
                    dve.wait_ge(s_mrow_loaded, upto(t + 1, 16))
                    dve.wait_ge(s_erow_made, upto(t))
                    dve.wait_ge(s_nmax_made, upto(t))
                    v.tensor_tensor(wrow[:, :], bank[7][0:PAIR, 0:P], mask_rows[:, :], ALU.mult
                                    ).then_inc(s_wrow_made, 1)
                    dve.wait_ge(s_wrow_made, upto(t + 1))
                    v.tensor_reduce(nmax[:, :], wrow[:, :], AX_X, ALU.max, negate=True).then_inc(s_nmax_made, 1)
                if live(3):
                    dve.wait_ge(s_AdT_mm, upto(t - 2))
                    dve.wait_ge(s_G_mm, upto(t - 3))
                    dve.wait_ge(s_bHT_made, upto(t - 3))
                    dve.wait_ge(s_cnt1_made, upto(t - 3))
                    for b in range(PAIR):
                        v.tensor_scalar(HT[:, b, :], small(3)[:, b, :], 0.0, 0.0, ALU.not_equal, ALU.add,
                                        accum_out=cnt[:, b:b + 1])
                    v.tensor_copy(wcol[:, :], small(3)[:, :, 0]).then_inc(s_HT_made, 1)
                if live(3):
                    dve.wait_ge(s_HT_made, upto(t - 2))
                    dve.wait_ge(s_binv_made, upto(t - 3))
                    v.tensor_scalar(cnt1[:, :], cnt[:, :], 1.0, None, ALU.max).then_inc(s_cnt1_made, 1)
                if live(3):
                    dve.wait_ge(s_cnt1_made, upto(t - 2))
                    dve.wait_ge(s_bHT_made, upto(t - 3))
                    v.reciprocal(binv[:, :], cnt1[:, :]).then_inc(s_binv_made, 1)
                if live(4):
                    dve.wait_ge(s_z_mm, upto(t - 3))
                    dve.wait_ge(s_Gz_mm, upto(t - 4))
                    v.tensor_tensor(z[:, :, :], halves(0), bw2[:, :].unsqueeze(1).broadcast_to([P, PAIR, D]),
                                    ALU.add).then_inc(s_z_out, 1)
                if live(0):
                    dve.wait_ge(s_prow_made, upto(t))
                    dve.wait_ge(s_erow_made, upto(t + 1))
                    v.reciprocal(einv[:, :], esum[:, :]).then_inc(s_einv_made, 1)
                    dve.wait_ge(s_einv_made, upto(t + 1))
                    dve.wait_ge(s_soft_mm, upto(t))
                    v.tensor_scalar(prow[:, :], erow[:, :], einv[:, :], None, ALU.mult).then_inc(s_prow_made, 1)
                if live(0):
                    dve.wait_ge(s_soft_mm, upto(t + 1))
                    dve.wait_ge(s_final[0], upto(t))
                    v.tensor_copy(soft[:, :], bank[7][:, 0:PAIR]).then_inc(s_soft_out, 1)
                if live(0):
                    dve.wait_ge(s_soft_out, upto(t + 1))
                    dve.wait_ge(s_V0_mm, upto(t + 1))
                    dve.wait_ge(s_x0_copied, upto(t + 1))
                    dve.wait_ge(s_xv1_made, upto(t))
                    dve.wait_ge(s_h[1], upto(t))
                    dve.wait_ge(s_stats[1], upto(t))
                    for b in range(PAIR):
                        last = v.scalar_tensor_tensor(X[1][:, b, :], halves(5)[:, b, :], soft[:, b:b + 1],
                                                      X[0][:, b, :], ALU.mult, ALU.add)
                    last.then_inc(s_final[0], 1)
                if live(0):
                    dve.wait_ge(s_final[0], upto(t + 1))
                    stats_of(1, t + 1, X[1])
                    aggregate(1, t + 1)
                if live(3):
                    dve.wait_ge(s_deg_mm, upto(t - 2))
                    dve.wait_ge(s_Dn_made, upto(t - 3))
                    v.tensor_copy(deg[:, :], bank[6][:, 256:256 + PAIR]).then_inc(s_deg_out, 1)
                if live(2):
                    dve.wait_ge(s_Ay_mm, upto(t - 1))
                    dve.wait_ge(s_ratio_made, upto(t - 1))
                    dve.wait_ge(s_xb3a_made, upto(t - 2))
                    dve.wait_ge(s_h[3], upto(t - 2))
                    dve.wait_ge(s_stats[3], upto(t - 2))
                    for b in range(PAIR):
                        last = v.scalar_tensor_tensor(X[3][:, b, :], halves(4)[:, b, :], ratio2[:, b:b + 1],
                                                      X[2][:, b, :], ALU.mult, ALU.add)
                    last.then_inc(s_final[2], 1)
                if live(1):
                    dve.wait_ge(s_inv1_made, upto(t))
                    dve.wait_ge(s_PV_mm, upto(t))
                    dve.wait_ge(s_xv1_made, upto(t))
                    dve.wait_ge(s_h[2], upto(t - 1))
                    dve.wait_ge(s_final[2], upto(t - 1))
                    dve.wait_ge(s_stats[2], upto(t - 1))
                    for b in range(PAIR):
                        last = v.scalar_tensor_tensor(X[2][:, b, :], halves(2)[:, b, :], inv1[:, b:b + 1],
                                                      xv1[:, b, :], ALU.mult, ALU.add)
                    last.then_inc(s_final[1], 1)
                if live(3):
                    dve.wait_ge(s_agg_hi, upto(t - 2))
                    v.tensor_tensor(aggT_lo[:, :, :, :].rearrange("p c b n -> p (c b n)"), bank[1][:, :],
                                    aggT_hi[:, :, :, :].bitcast(F32).rearrange("p c b n -> p (c b n)"), ALU.subtract
                                    ).then_inc(s_agg_lo, 1)
                if live(1):
                    dve.wait_ge(s_final[1], upto(t))
                    stats_of(2, t, X[2])
                    aggregate(2, t)
                if live(4):
                    dve.wait_ge(s_Dn_made, upto(t - 3))
                    dve.wait_ge(s_Gz_mm, upto(t - 3))
                    dve.wait_ge(s_xb3_made, upto(t - 3))
                    dve.wait_ge(s_x_stored, upto(t - 4, 16))
                    for b in range(PAIR):
                        last = v.scalar_tensor_tensor(x_out[:, b, :], halves(0)[:, b, :], Dn[:, b:b + 1],
                                                      xb3[:, b, :], ALU.mult, ALU.add)
                    last.then_inc(s_final[3], 1)
                if live(3):
                    dve.wait_ge(s_deg_out, upto(t - 2))
                    v.tensor_scalar(deg1[:, :], deg[:, :], TINY, None, ALU.max).then_inc(s_deg1_made, 1)
                    dve.wait_ge(s_deg1_made, upto(t - 2))
                    v.reciprocal(dinv[:, :], deg1[:, :]).then_inc(s_dinv_made, 1)
                    dve.wait_ge(s_dinv_made, upto(t - 2))
                    dve.wait_ge(s_final[3], upto(t - 3))
                    dve.wait_ge(s_o1_made[1], upto(t - 3))
                    v.scalar_tensor_tensor(Dn[:, :], deg[:, :], 0.0, dinv[:, :], ALU.is_gt, ALU.mult
                                           ).then_inc(s_Dn_made, 1)
                if live(3):
                    for b in range(PAIR):
                        dve.wait_ge(s_O1_mm[b], upto(t - 2))
                        dve.wait_ge(s_Dn_made, upto(t - 2))
                        dve.wait_ge(s_r3_made[b], upto(t - 3))
                        v.scalar_tensor_tensor(o1[:, b, :], bank[3 + b][:, :], Dn[:, b:b + 1],
                                               b1_bc[:, :], ALU.mult, ALU.add).then_inc(s_o1_made[b], 1)

            steps(dve, step)

        @block.tensor
        def _(pe):
            mm = nc.tensor.matmul

            def turn(dst, src):
                return nc.tensor.transpose(dst, src, ident[:, :])

            def product(dst, terms):
                for i, (a, b) in enumerate(terms):
                    last = mm(dst, a, b, start=(i == 0), stop=(i == len(terms) - 1))
                return last

            def split_product(dst, terms):
                return product(dst, [(x, y) for (ah, al), (bh, bl) in terms
                                     for x, y in ((ah, bl), (al, bh), (ah, bh))])

            pe.wait_ge(s_ident_made, 1)
            pe.wait_ge(s_reps_made, 1)
            pe.wait_ge(s_w_loaded, 16 * 8)
            def blocks(b, src, rows, cols):
                i = 0
                for c in cols:
                    for r in rows:
                        last = turn(bank[b][:, i * P:(i + 1) * P], src[:, r, c * P:(c + 1) * P])
                        i += 1
                return last
            def chunk(c):
                return slice(c * P, (c + 1) * P)
            blocks(0, rwqk0, range(C), range(0, C)).then_inc(s_wturned, 1)
            blocks(1, rwqk0, range(C), range(C, 2 * C)).then_inc(s_wturned, 1)
            blocks(2, rwv1, range(C), range(C)).then_inc(s_wturned, 1)
            blocks(3, rw2, range(C), range(C)).then_inc(s_wturned, 1)
            blocks(4, rw31, range(K), range(0, 1)).then_inc(s_wturned, 1)
            blocks(5, rw31, range(K), range(1, 2)).then_inc(s_wturned, 1)
            blocks(6, rw32, range(C), range(0, 2)).then_inc(s_wturned, 1)
            blocks(7, rw32, range(C), range(2, 4)).then_inc(s_wturned, 1)
            pe.wait_ge(s_turned_out, 8)
            for c in range(C):
                last = product(halves(0)[:, c, :], [(wq0_t[:, a, chunk(c)], wk0_t[:, a, :]) for a in range(C)])
            last.then_inc(s_wturned, 1)
            for c in range(C):
                last = product(halves(1)[:, c, :], [(rwq1[:, a, chunk(c)], rwk1[:, a, :]) for a in range(C)])
            last.then_inc(s_wturned, 1)
            for c in range(C):
                last = product(small(2)[:, c, :], [(w2_t[:, a, chunk(c)], a_rep[:, a, :]) for a in range(C)])
            last.then_inc(s_wturned, 1)
            for c in range(C):
                product(bank[3][:, c:c + 1], [(rwk1[:, a, chunk(c)], bq_col[:, a:a + 1]) for a in range(C)])
                product(bank[3][:, 2 + c:3 + c], [(rwq1[:, a, chunk(c)], bk_col[:, a:a + 1]) for a in range(C)])
            product(bank[3][:, 4:5], [(bq_rep[:, a, :], bk_col[:, a:a + 1]) for a in range(C)]).then_inc(s_wturned, 1)
            product(bank[4][:, 0:D], [(beta_rep[:, k, :], w32_t[:, k, :]) for k in range(K)]).then_inc(s_wturned, 1)
            pe.wait_ge(s_turned_out, TURNS)
            pe.wait_ge(s_split_done, 1)

            def turn_pair(b, src):
                for c in range(C):
                    for g in range(PAIR):
                        last = turn(quarters(b)[:, c, g, :], src[:, g, chunk(c)])
                return last

            def mix(b, w, l):
                for m in range(C):
                    last = split_product(bank[b][:, m * 256:(m + 1) * 256],
                                         [((w[0][:, c, chunk(m)], w[1][:, c, chunk(m)]),
                                           (hT_hi[l][:, c, :, :], hT_lo[l][:, c, :, :])) for c in range(C)])
                return last

            def project(b, w, l):
                for g in range(PAIR):
                    last = split_product(halves(b)[:, g, :],
                                         [((hT_hi[l][:, c, g, :], hT_lo[l][:, c, g, :]),
                                           (w[0][:, c, :], w[1][:, c, :])) for c in range(C)])
                return last

            def scores(b, left, l):
                for g in range(PAIR):
                    last = product(small(b)[:, g, :], [(left[:, c, g, :], hT[l][:, c, g, :]) for c in range(C)])
                return last

            def step(t, live):
                if live(1):
                    pe.wait_ge(s_h[1], upto(t))
                    pe.wait_ge(s_agg_lo, upto(t - 3))
                    turn_pair(1, H[1]).then_inc(s_turned[1], 1)
                if live(2):
                    pe.wait_ge(s_h[2], upto(t - 1))
                    pe.wait_ge(s_final[1], upto(t - 1))
                    turn_pair(2, H[2]).then_inc(s_turned[2], 1)
                if live(0):
                    pe.wait_ge(s_lo[0], upto(t + 1))
                    pe.wait_ge(s_final[3], upto(t - 4))
                    mix(0, m0_p, 0).then_inc(s_tT_mm, 1)
                if live(1):
                    pe.wait_ge(s_lo[1], upto(t))
                    pe.wait_ge(s_final[0], upto(t))
                    mix(5, m1_p, 1).then_inc(s_uT_mm, 1)
                if live(2):
                    pe.wait_ge(s_lo[2], upto(t - 1))
                    pe.wait_ge(s_tT_out, upto(t + 1))
                    split_product(bank[0][:, 0:256],
                                  [((wa_p[0][:, c, :], wa_p[1][:, c, :]),
                                    (hT_hi[2][:, c, :, :], hT_lo[2][:, c, :, :])) for c in range(C)]
                                  ).then_inc(s_sb_mm, 1)
                if live(1):
                    pe.wait_ge(s_lo[2], upto(t - 1))
                    pe.wait_ge(s_soft_out, upto(t))
                    for g in range(PAIR):
                        last = split_product(bank[VBANK[g]][:, 0:DV],
                                             [((hT_hi[1][:, c, g, :], hT_lo[1][:, c, g, :]),
                                               (wv1_p[0][:, c, :], wv1_p[1][:, c, :])) for c in range(C)])
                    last.then_inc(s_V1_mm, 1)
                if live(2):
                    pe.wait_ge(s_lo[0], upto(t + 1))
                    project(6, w2_p, 2).then_inc(s_y_mm, 1)
                if live(1):
                    pe.wait_ge(s_full[1], upto(t))
                    pe.wait_ge(s_uT_out, upto(t))
                    scores(1, uT, 1).then_inc(s_S1_mm, 1)
                if live(4):
                    pe.wait_ge(s_h1n_made, upto(t - 3))
                    for g in range(PAIR):
                        for k in range(K):
                            last = turn(bank[3 + g][:, k * P:(k + 1) * P], h1n[:, g, chunk(k)])
                        last.then_inc(s_h1T_mm[g], 1)
                if live(0):
                    pe.wait_ge(s_tT_out, upto(t + 1))
                    pe.wait_ge(s_e1_made, upto(t))
                    scores(1, tT, 0).then_inc(s_S0_mm, 1)
                if live(1):
                    pe.wait_ge(s_p1_made, upto(t))
                    pe.wait_ge(s_y_out, upto(t - 1))
                    for g in range(PAIR):
                        last = turn(small(6)[:, g, :], p1[:, g, :])
                    last.then_inc(s_PT_mm, 1)
                if live(2):
                    pe.wait_ge(s_a2_made, upto(t - 1))
                    pe.wait_ge(s_y_out, upto(t - 1))
                    for g in range(PAIR):
                        last = turn(bank[6][:, (2 + g) * P:(3 + g) * P], a2m[:, g, :])
                    last.then_inc(s_AT_mm, 1)
                for g in range(PAIR):
                    if live(4):
                        pe.wait_ge(s_h1T_lo[g], upto(t - 3))
                        pe.wait_ge(s_tanh_made, upto(t - 1))
                        last = split_product(halves(0)[:, g, :],
                                             [((h1T_hi[:, g, k, :], h1T_lo[:, g, k, :]),
                                               (w32_p[0][:, k, :], w32_p[1][:, k, :])) for k in range(K)])
                        if g == PAIR - 1:
                            last.then_inc(s_z_mm, 1)
                    if live(0) and g == 0:
                        pe.wait_ge(s_w0_made, upto(t + 1))
                        pe.wait_ge(s_r1_out, upto(t))
                        product(bank[7][0:PAIR, 0:P], [(w0[:, :], ident[:, :])]).then_inc(s_wT_mm, 1)
                    if live(3) and g == 0:
                        pe.wait_ge(s_a3_loaded, upto(t - 2, 16))
                        pe.wait_ge(s_h1T_lo[0], upto(t - 3))
                        for b in range(PAIR):
                            last = turn(small(3)[:, b, :], AD[3][:, b, :])
                        last.then_inc(s_AdT_mm, 1)
                if live(0):
                    pe.wait_ge(s_uT_out, upto(t))
                    project(5, wv0_p, 0).then_inc(s_V0_mm, 1)
                    pe.wait_ge(s_prow_made, upto(t + 1))
                    product(bank[7][:, 0:PAIR], [(prow[:, :], ident[0:PAIR, 0:PAIR])]).then_inc(s_soft_mm, 1)
                if live(4):
                    pe.wait_ge(s_z_out, upto(t - 3))
                    for g in range(PAIR):
                        last = product(halves(0)[:, g, :], [(G[:, g, :], z[:, g, :])])
                    last.then_inc(s_Gz_mm, 1)
                if live(3):
                    pe.wait_ge(s_bHT_made, upto(t - 2))
                    pe.wait_ge(s_h1T_lo[1], upto(t - 3))
                    for g in range(PAIR):
                        last = product(small(4)[:, g, :], [(HT[:, g, :], bHT[:, g, :])])
                    last.then_inc(s_G_mm, 1)
                    pe.wait_ge(s_HT_made, upto(t - 2))
                    pe.wait_ge(s_PT_out, upto(t))
                    pe.wait_ge(s_AT_out, upto(t - 1))
                    for g in range(PAIR):
                        last = product(bank[6][:, 256 + g:257 + g], [(HT[:, g, :], wcol[:, g:g + 1])])
                    last.then_inc(s_deg_mm, 1)
                if live(1):
                    pe.wait_ge(s_PT_out, upto(t))
                    pe.wait_ge(s_V1_out, upto(t))
                    pe.wait_ge(s_r1_out, upto(t))
                    for g in range(PAIR):
                        last = product(halves(2)[:, g, :], [(p1T[:, g, :], v1[:, g, :])])
                    last.then_inc(s_PV_mm, 1)
                if live(2):
                    pe.wait_ge(s_AT_out, upto(t - 1))
                    pe.wait_ge(s_G_out, upto(t - 2))
                    for g in range(PAIR):
                        last = product(halves(4)[:, g, :], [(a2T[:, g, :], y2[:, g, :])])
                    last.then_inc(s_Ay_mm, 1)
                if live(3):
                    pe.wait_ge(s_G_out, upto(t - 2))
                    pe.wait_ge(s_h[3], upto(t - 2))
                    pe.wait_ge(s_w0_made, upto(t + 1))
                    for g in range(PAIR):
                        for c in range(C):
                            last = product(quarters(1)[:, c, g, :], [(H[3][:, g, chunk(c)], G[:, g, :])])
                    last.then_inc(s_agg_mm, 1)
                if live(-1):
                    pe.wait_ge(s_h[0], upto(t + 2))
                    pe.wait_ge(s_deg_out, upto(t - 2))
                    turn_pair(6, H[0]).then_inc(s_turned[0], 1)
                if live(3):
                    for g in range(PAIR):
                        pe.wait_ge(s_agg_lo, upto(t - 2))
                        pe.wait_ge(s_HT_made, upto(t - 2))
                        pe.wait_ge(s_final[2], upto(t - 1))
                        for j in range(DH // 256):
                            cols = slice(j * 256, (j + 1) * 256)
                            last = split_product(bank[3 + g][:, cols],
                                                 [((aggT_hi[:, c, g, :], aggT_lo[:, c, g, :]),
                                                   (w31_p[0][:, c, cols], w31_p[1][:, c, cols])) for c in range(C)])
                        last.then_inc(s_O1_mm[g], 1)

            steps(pe, step)


_INS = ["x", "adj", "nodemask", "L0_gnn_Wqk", "L0_gnn_Wv", "L1_gnn_Wq_w", "L1_gnn_Wq_b", "L1_gnn_Wk_w",
        "L1_gnn_Wk_b", "L1_gnn_Wv_w", "L1_gnn_Wv_b", "L2_gnn_w", "L2_gnn_a", "L3_gnn_W1", "L3_gnn_b1",
        "L3_gnn_gamma", "L3_gnn_beta", "L3_gnn_W2", "L3_gnn_b2"]


def kernel(**inputs):
    import numpy as np
    import concourse.bacc as bacc
    from concourse.bass_utils import run_bass_kernel_spmd as run

    nc = bacc.Bacc("TRN2", target_bir_lowering=False, num_devices=1)
    arrays, args = {}, []
    for name in _INS:
        a = np.ascontiguousarray(inputs[name])
        arrays[f"in_{name}_dram"] = a
        args.append(nc.dram_tensor(f"in_{name}_dram", a.shape, mybir.dt.from_np(a.dtype), kind="ExternalInput").ap())
    out = nc.dram_tensor("out_dram", arrays["in_x_dram"].shape, F32, kind="ExternalOutput").ap()
    build(nc, *args, out)
    return run(nc, [arrays], core_ids=[0]).results[0]["out_dram"]
```

```python
from contextlib import ExitStack

import concourse.bass as bass
from concourse import mybir

F32 = mybir.dt.float32
F32R = mybir.dt.float32r
ALU = mybir.AluOpType
ACT = mybir.ActivationFunctionType
AX_X = mybir.AxisListType.X

P = 128
PAIR = 2
EPS = 1e-5
TINY = 1.2e-38
AHEAD = 1
LAST_OFF = 5


def build(nc, x, adj, mask, wqk0, wv0, wq1, bq1, wk1, bk1, wv1, bv1, w2, a2, w31, b31, gamma, beta,
          w32, b32, out):
    B, N, D = x.shape
    NG = B // PAIR
    C = D // P
    DH = w31.shape[0]
    K = DH // P
    assert N == P and C == 2 and K == 4
    INV = float(D) ** -0.5

    with ExitStack() as ctx:
        def sb(name, shape, dt=F32):
            return ctx.enter_context(nc.sbuf_tensor(name, shape, dt))

        def sem(name):
            return ctx.enter_context(nc.semaphore(name))

        bank = [ctx.enter_context(nc.psum_tensor(f"bank{i}", [P, 512], F32)) for i in range(8)]

        def quarters(b):
            return bank[b][:, :].rearrange("p (c b n) -> p c b n", c=2, b=2)

        def halves(b):
            return bank[b][:, :].rearrange("p (b d) -> p b d", b=2)

        def small(b):
            return bank[b][:, 0:256].rearrange("p (b d) -> p b d", b=2)

        gram = bank[5][:, 0:PAIR * (P + 1)].rearrange("p (b n) -> p b n", b=PAIR)

        ident = sb("ident", [P, P])
        rwqk0, rwv0 = sb("rwqk0", [P, C, 2 * D]), sb("rwv0", [P, C, D])
        rwq1, rwk1, rwv1 = sb("rwq1", [P, C, D]), sb("rwk1", [P, C, D]), sb("rwv1", [P, C, D])
        rw2, rw31, rw32 = sb("rw2", [P, C, D]), sb("rw31", [P, K, D]), sb("rw32", [P, C, DH])
        bq_col, bk_col, a_col = sb("bq_col", [P, C]), sb("bk_col", [P, C]), sb("a_col", [P, C])
        gamma_col, beta_col = sb("gamma_col", [P, K]), sb("beta_col", [P, K])
        bv_bc, b1_bc, b2_bc = sb("bv_bc", [P, D]), sb("b1_bc", [P, DH]), sb("b2_bc", [P, D])
        ones = sb("ones", [P, P])
        a_rep, beta_rep = sb("a_rep", [P, C, P]), sb("beta_rep", [P, K, P])
        bq_rep = sb("bq_rep", [P, C, P])
        wq0_t, wk0_t, w2_t = (sb(n, [P, C, D]) for n in ("wq0_t", "wk0_t", "w2_t"))
        DV = D + 2
        wv1_t = sb("wv1_t", [P, C, DV])
        w31_t, w32_t, w32_g = sb("w31_t", [P, C, DH]), sb("w32_t", [P, K, D]), sb("w32_g", [P, K, D])
        m0, m1 = sb("m0", [P, C, D]), sb("m1", [P, C, D])
        wa = sb("wa", [P, C, P])
        vecs = sb("vecs", [P, 5])
        bw2 = sb("bw2", [P, D])
        ubias, rconst = vecs[:, 0:2], vecs[:, 4:5]

        def parts(name, shape):
            return sb(name + "_hi", shape, F32R), sb(name + "_lo", shape, F32R)

        m0_p, m1_p, wv0_p, w2_p = (parts(n, [P, C, D]) for n in ("pm0", "pm1", "pwv0", "pw2"))
        wv1_p = parts("pwv1", [P, C, DV])
        wa_p = parts("pwa", [P, C, P])
        w31_p, w32_p = parts("pw31", [P, C, DH]), parts("pw32", [P, K, D])

        x_in = sb("x_in", [P, PAIR, D])
        X = [sb(f"X{l}", [P, PAIR, D]) for l in range(4)]
        x_out = sb("x_out", [P, PAIR, D])
        H = [sb(f"H{l}", [P, PAIR, D]) for l in range(4)]
        stats = [sb(f"stats{l}", [P, PAIR, 6]) for l in range(5)]
        mv = [sb(f"mv{l}", [P, PAIR, 2]) for l in range(5)]
        vare = [sb(f"vare{l}", [P, PAIR, 1]) for l in range(5)]
        rstd = [sb(f"rstd{l}", [P, PAIR, 1]) for l in range(5)]
        nmean = [sb(f"nmean{l}", [P, PAIR, 1]) for l in range(4)]
        nmr = [sb(f"nmr{l}", [P, PAIR, 1]) for l in range(4)]
        eps_t, half_t, neg_t = sb("eps_t", [P, PAIR, 1]), sb("half_t", [P, PAIR, 1]), sb("neg_t", [P, PAIR, 1])
        dve_scratch = sb("dve_scratch", [P, 5])
        hT_hi = [sb(f"hT{l}_hi", [P, C, PAIR, P], F32R) for l in range(3)]
        hT_lo = [sb(f"hT{l}_lo", [P, C, PAIR, P], F32R) for l in range(3)]
        hT = [sb(f"hT{l}", [P, C, PAIR, P]) for l in range(2)]
        AD = [sb(f"AD{l}", [P, PAIR, P]) for l in range(4)]
        mask_bc = sb("mask_bc", [P, PAIR, P])
        mask_rows = sb("mask_rows", [PAIR, P])
        adm = sb("adm", [P, PAIR, P])
        tT, uT = sb("tT", [P, C, PAIR, P]), sb("uT", [P, C, PAIR, P])
        junk, junk0 = sb("junk", [P, PAIR, P]), sb("junk0", [P, PAIR, P])
        w0 = sb("w0", [P, PAIR])
        wrow, erow, prow = (sb(n, [PAIR, P]) for n in ("wrow", "erow", "prow"))
        nmax, esum, einv = (sb(n, [PAIR, 1]) for n in ("nmax", "esum", "einv"))
        soft = sb("soft", [P, PAIR])
        r1 = sb("r1", [P, PAIR])
        e1, p1, p1T = sb("e1", [P, PAIR, P]), sb("p1", [P, PAIR, P]), sb("p1T", [P, PAIR, P])
        v1, xv1 = sb("v1", [P, PAIR, D]), sb("xv1", [P, PAIR, D])
        sum1, inv1 = sb("sum1", [P, PAIR]), sb("inv1", [P, PAIR])
        s2 = sb("s2", [P, PAIR])
        th2, lr2, e2 = (sb(n, [P, PAIR, P]) for n in ("th2", "lr2", "e2"))
        a2m, a2T = sb("a2m", [P, PAIR, P]), sb("a2T", [P, PAIR, P])
        sum2, inv2, asum2, ratio2 = (sb(n, [P, PAIR]) for n in ("sum2", "inv2", "asum2", "ratio2"))
        y2 = sb("y2", [P, PAIR, D])
        HT = sb("HT", [P, PAIR, P])
        bHT, G = sb("bHT", [P, PAIR, P + 1]), sb("G", [P, PAIR, P + 1])
        G_kept = sb("G_kept", [P, PAIR, P])
        cnt, cnt1, binv = (sb(n, [P, PAIR]) for n in ("cnt", "cnt1", "binv"))
        deg1, dinv, Dn = (sb(n, [P, PAIR]) for n in ("deg1", "dinv", "Dn"))
        aggT_hi, aggT_lo = parts("aggT", [P, C, PAIR, P])
        o1, r3, h1n = (sb(n, [P, PAIR, DH]) for n in ("o1", "r3", "h1n"))
        h1T_hi, h1T_lo = parts("h1T", [P, PAIR, K, P])
        z = sb("z", [P, PAIR, D])
        xb3a, xb3 = sb("xb3a", [P, PAIR, D]), sb("xb3", [P, PAIR, D])

        s_wqk0_loaded = sem("s_wqk0_loaded")
        s_wqk1_loaded = sem("s_wqk1_loaded")
        s_w3_loaded = sem("s_w3_loaded")
        s_wv1_loaded = sem("s_wv1_loaded")
        s_w2_loaded = sem("s_w2_loaded")
        s_wv0_loaded = sem("s_wv0_loaded")
        s_cols_loaded = sem("s_cols_loaded")
        s_b_loaded = sem("s_b_loaded")
        s_ident_made = sem("s_ident_made")
        s_reps_made = sem("s_reps_made")
        s_consts = sem("s_consts")
        s_wturned = sem("s_wturned")
        s_turned_out = sem("s_turned_out")
        s_hi_done = sem("s_hi_done")
        s_lo_vector = sem("s_lo_vector")
        s_lo_pool = sem("s_lo_pool")
        s_x_loaded = sem("s_x_loaded")
        s_x_stored = sem("s_x_stored")
        s_mbc_loaded = sem("s_mbc_loaded")
        s_mrow_loaded = sem("s_mrow_loaded")
        s_a0_loaded = sem("s_a0_loaded")
        s_a1_loaded = sem("s_a1_loaded")
        s_a2_loaded = sem("s_a2_loaded")
        s_a3_loaded = sem("s_a3_loaded")
        s_x0_copied = sem("s_x0_copied")
        s_adm_made = sem("s_adm_made")
        s_tT_mm = sem("s_tT_mm")
        s_tT_out = sem("s_tT_out")
        s_S0_mm = sem("s_S0_mm")
        s_w0_made = sem("s_w0_made")
        s_wT_mm = sem("s_wT_mm")
        s_wrow_made = sem("s_wrow_made")
        s_nmax_made = sem("s_nmax_made")
        s_erow_made = sem("s_erow_made")
        s_einv_made = sem("s_einv_made")
        s_prow_made = sem("s_prow_made")
        s_soft_mm = sem("s_soft_mm")
        s_soft_out = sem("s_soft_out")
        s_V0_mm = sem("s_V0_mm")
        s_uT_mm = sem("s_uT_mm")
        s_uT_out = sem("s_uT_out")
        s_r1_out = sem("s_r1_out")
        s_S1_mm = sem("s_S1_mm")
        s_e1_made = sem("s_e1_made")
        s_p1_made = sem("s_p1_made")
        s_inv1_made = sem("s_inv1_made")
        s_PT_mm = sem("s_PT_mm")
        s_PT_out = sem("s_PT_out")
        s_V1_mm = sem("s_V1_mm")
        s_V1_out = sem("s_V1_out")
        s_PV_mm = sem("s_PV_mm")
        s_xv1_made = sem("s_xv1_made")
        s_sb_mm = sem("s_sb_mm")
        s_s2_made = sem("s_s2_made")
        s_tanh_made = sem("s_tanh_made")
        s_lr_made = sem("s_lr_made")
        s_e2_made = sem("s_e2_made")
        s_a2_made = sem("s_a2_made")
        s_inv2_made = sem("s_inv2_made")
        s_ratio_made = sem("s_ratio_made")
        s_AT_mm = sem("s_AT_mm")
        s_AT_out = sem("s_AT_out")
        s_y_mm = sem("s_y_mm")
        s_y_out = sem("s_y_out")
        s_Ay_mm = sem("s_Ay_mm")
        s_AdT_mm = sem("s_AdT_mm")
        s_HT_made = sem("s_HT_made")
        s_cnt1_made = sem("s_cnt1_made")
        s_binv_made = sem("s_binv_made")
        s_bHT_made = sem("s_bHT_made")
        s_deg1_made = sem("s_deg1_made")
        s_dinv_made = sem("s_dinv_made")
        s_Dn_made = sem("s_Dn_made")
        s_G_mm = sem("s_G_mm")
        s_G_out = sem("s_G_out")
        s_G_kept = sem("s_G_kept")
        s_agg_mm = sem("s_agg_mm")
        s_agg_hi = sem("s_agg_hi")
        s_agg_lo = sem("s_agg_lo")
        s_O1_mm = [sem(f"s_O1_mm{g}") for g in range(PAIR)]
        s_o1_made = [sem(f"s_o1_made{g}") for g in range(PAIR)]
        s_r3_made = [sem(f"s_r3_made{g}") for g in range(PAIR)]
        s_h1n_made = sem("s_h1n_made")
        s_h1T_mm = [sem(f"s_h1T_mm{g}") for g in range(PAIR)]
        s_h1T_hi = [sem(f"s_h1T_hi{g}") for g in range(PAIR)]
        s_h1T_lo = [sem(f"s_h1T_lo{g}") for g in range(PAIR)]
        s_z_mm = sem("s_z_mm")
        s_z_out = sem("s_z_out")
        s_Gz_mm = sem("s_Gz_mm")
        s_xb3a_made = sem("s_xb3a_made")
        s_xb3_made = sem("s_xb3_made")
        s_stats = [sem(f"s_stats{l}") for l in range(5)]
        s_mv = [sem(f"s_mv{l}") for l in range(5)]
        s_vare = [sem(f"s_vare{l}") for l in range(5)]
        s_rstd = [sem(f"s_rstd{l}") for l in range(5)]
        s_terms = [sem(f"s_terms{l}") for l in range(4)]
        s_nmean = [sem(f"s_nmean{l}") for l in range(4)]
        s_h = [sem(f"s_h{l}") for l in range(4)]
        s_turned = [sem(f"s_turned{l}") for l in range(3)]
        s_hi = [sem(f"s_hi{l}") for l in range(3)]
        s_lo = [sem(f"s_lo{l}") for l in range(3)]
        s_full = [sem(f"s_full{l}") for l in range(2)]
        s_final = [sem(f"s_final{l}") for l in range(4)]

        def upto(n, unit=1):
            return (min(max(n, 0), NG) if isinstance(n, int) else n) * unit

        turn_jobs = [(wq0_t[:, :, :], 512), (wk0_t[:, :, :], 512), (m1[:, :, :], 512), (m0[:, :, :], 512),
                     (w31_t[:, 0, :], 512), (w31_t[:, 1, :], 512), (vecs[:, :], "vecs"), (w2_t[:, :, :], 512),
                     (wv1_t[:, :, 0:D], 512), (0, "gamma"), (2, "gamma"), (wa[:, :, :], 256), (bw2[:, :], 256)]
        TURNS = len(turn_jobs)
        EARLY_TURNS = 11
        TURN_BANKS = (0, 1, 2, 3, 4, 5, 7, 2, 3, 4, 6, 2, 3)
        splits = [(m0, m0_p, s_turned_out, 4, "vector"), (rwv0, wv0_p, s_wv0_loaded, 16, "pool"),
                  (m1, m1_p, s_turned_out, 3, "pool"), (w31_t, w31_p, s_turned_out, 6, "vector"),
                  (rw2, w2_p, s_w2_loaded, 16, "pool"), (wv1_t, wv1_p, s_turned_out, 9, "vector"),
                  (w32_g, w32_p, s_turned_out, 11, "vector"), (wa, wa_p, s_turned_out, 12, "pool")]
        EARLY_SPLITS = 6
        LO_POOL = sum(who == "pool" for *_, who in splits)
        LO_VECTOR = len(splits) - LO_POOL
        VBANK = [2, 7]
        TBANK = [6, 1, 3]

        FIRST, LAST = LAST_OFF, NG - 1 - AHEAD

        def steps(eng, step, setup, late=None, early=None):
            if early:
                early()
            for t in range(-AHEAD, 0):
                step(t, lambda off, t=t: 0 <= t - off < NG)
            setup()
            for t in range(0, 1):
                step(t, lambda off, t=t: 0 <= t - off < NG)
            if late:
                late()
            for t in range(1, FIRST):
                step(t, lambda off, t=t: 0 <= t - off < NG)
            with eng.Fori(FIRST, LAST + 1) as t:
                step(t, lambda off: True)
            for t in range(LAST + 1, NG + LAST_OFF):
                step(t, lambda off, t=t: 0 <= t - off < NG)

        block = ctx.enter_context(nc.Block())

        @block.sync
        def _(sp):
            def rows(v, g):
                return v[bass.ds(g * PAIR, PAIR)] if not isinstance(g, int) else v[g * PAIR:(g + 1) * PAIR]

            def load(dst, src, g, signal, free, n):
                sp.wait_ge(free, upto(n))
                sp.dma_start(dst[:, :, :], rows(src, g).rearrange("b p d -> p b d")).then_inc(signal, 16)

            def setup():
                def weight(dst, src, loaded):
                    sp.dma_start(dst[:, :, :], src.rearrange("(c p) n -> p c n", p=P)).then_inc(loaded, 16)

                def column(dst, src):
                    sp.dma_start(dst[:, :], src.rearrange("(c p) -> p c", p=P), allow_slow_non_contiguous=True
                                 ).then_inc(s_cols_loaded, 16)

                def bias_rows(dst, src):
                    sp.dma_start(dst[:, :], src.unsqueeze(0).broadcast_to([P, dst.shape[1]])
                                 ).then_inc(s_b_loaded, 16)

                weight(rwqk0, wqk0, s_wqk0_loaded)
                weight(rwq1, wq1, s_wqk1_loaded)
                weight(rwk1, wk1, s_wqk1_loaded)
                weight(rw31, w31, s_w3_loaded)
                column(bq_col, bq1)
                column(bk_col, bk1)
                column(a_col, a2)
                column(beta_col, beta)
                column(gamma_col, gamma)
                weight(rwv0, wv0, s_wv0_loaded)
                weight(rw32, w32, s_w3_loaded)
                weight(rwv1, wv1, s_wv1_loaded)
                weight(rw2, w2, s_w2_loaded)
                bias_rows(bv_bc, bv1)
                bias_rows(b1_bc, b31)
                bias_rows(b2_bc, b32)

            def step(t, live):
                if live(0):
                    load(AD[0], adj, t, s_a0_loaded, s_adm_made, t)
                if live(0):
                    sp.dma_start(mask_bc[:, :, :], rows(mask, t).unsqueeze(0).broadcast_to([P, PAIR, P])
                                 ).then_inc(s_mbc_loaded, 16)
                if live(0):
                    sp.wait_ge(s_wrow_made, upto(t))
                    sp.dma_start(mask_rows[:, :], rows(mask, t)).then_inc(s_mrow_loaded, 16)
                if live(1):
                    load(AD[1], adj, t - 1, s_a1_loaded, s_p1_made, t - 1)
                if live(2):
                    load(AD[2], adj, t - 2, s_a2_loaded, s_a2_made, t - 2)
                if live(3):
                    load(AD[3], adj, t - 3, s_a3_loaded, s_AdT_mm, t - 3)
                if live(-1):
                    load(x_in, x, t + 1, s_x_loaded, s_x0_copied, t + 1)

            steps(sp, step, setup)

        @block.gpsimd
        def _(pool):
            gp = nc.gpsimd
            gp.memset(ident[:, :], 0.0).then_inc(s_consts, 1)
            gp.memset(ones[:, :], 1.0)
            gp.memset(eps_t[:, :, :], EPS)
            gp.memset(wv1_t[:, :, D + 1], 0.0)
            gp.memset(half_t[:, :, :], -0.5)
            gp.memset(neg_t[:, :, :], -1.0).then_inc(s_consts, 1)
            pool.wait_ge(s_consts, 2)
            gp.affine_select(out=ident[:, :], in_=ident[:, :], compare_op=ALU.not_equal, fill=1.0,
                             base=0, pattern=[[-1, P]], channel_multiplier=1).then_inc(s_ident_made, 1)
            def rstd_of(l, n, used):
                pool.wait_ge(s_mv[l], upto(n))
                gp.tensor_tensor(vare[l][:, :, :], mv[l][:, :, 1:2], eps_t[:, :, :], ALU.add
                                 ).then_inc(s_vare[l], 1)
                pool.wait_ge(s_vare[l], upto(n))
                gp.tensor_tensor(rstd[l][:, :, :], vare[l][:, :, :], half_t[:, :, :], ALU.pow
                                 ).then_inc(s_rstd[l], 1)

            def norm_terms(l, n, used):
                rstd_of(l, n, used)
                gp.tensor_tensor(nmean[l][:, :, :], mv[l][:, :, 0:1], neg_t[:, :, :], ALU.mult).then_inc(s_nmean[l], 1)
                pool.wait_ge(s_nmean[l], upto(n))
                pool.wait_ge(s_rstd[l], upto(n))
                gp.tensor_tensor(nmr[l][:, :, :], nmean[l][:, :, :], rstd[l][:, :, :], ALU.mult
                                 ).then_inc(s_terms[l], 1)

            def bc(v):
                return v[:, :].unsqueeze(1).broadcast_to([P, PAIR, D])

            def step(t, live):
                if live(2):
                    norm_terms(2, t - 1, s_h[2])
                if live(0):
                    pool.wait_ge(s_a0_loaded, upto(t + 1, 16))
                    pool.wait_ge(s_mbc_loaded, upto(t + 1, 16))
                    gp.tensor_tensor(adm[:, :, :], AD[0][:, :, :], mask_bc[:, :, :], ALU.mult
                                     ).then_inc(s_adm_made, 1)
                if live(4):
                    pool.wait_ge(s_xb3a_made, upto(t - 3))
                    pool.wait_ge(s_h[3], upto(t - 3))
                    pool.wait_ge(s_final[3], upto(t - 4))
                    gp.tensor_tensor(xb3[:, :, :], xb3a[:, :, :], H[3][:, :, :], ALU.add).then_inc(s_xb3_made, 1)
                if live(1):
                    pool.wait_ge(s_lo[1], upto(t))
                    gp.tensor_tensor(hT[1][:, :, :, :], hT_hi[1][:, :, :, :].bitcast(F32),
                                     hT_lo[1][:, :, :, :].bitcast(F32), ALU.add).then_inc(s_full[1], 1)
                if live(4):
                    rstd_of(4, t - 3, s_h1n_made)
                if live(3):
                    pool.wait_ge(s_final[2], upto(t - 2))
                    gp.tensor_tensor(xb3a[:, :, :], X[3][:, :, :], bc(b2_bc), ALU.add).then_inc(s_xb3a_made, 1)
                if live(3):
                    norm_terms(3, t - 2, s_h[3])
                if live(1):
                    pool.wait_ge(s_final[0], upto(t))
                    gp.tensor_tensor(xv1[:, :, :], X[1][:, :, :], bc(bv_bc), ALU.add).then_inc(s_xv1_made, 1)
                if live(-1):
                    norm_terms(0, t + 2, s_h[0])
                if live(0):
                    norm_terms(1, t + 1, s_h[1])
                if live(-1):
                    pool.wait_ge(s_full[0], upto(t + 2))
                    pool.wait_ge(s_hi[0], upto(t + 2))
                    gp.tensor_tensor(hT_lo[0][:, :, :, :], hT[0][:, :, :, :], hT_hi[0][:, :, :, :].bitcast(F32),
                                     ALU.subtract).then_inc(s_lo[0], 1)

            def low_parts(first, end):
                for i in range(first, end):
                    whole, (hi, lo), _, _, who = splits[i]
                    if who == "pool":
                        pool.wait_ge(s_hi_done, i + 1)
                        gp.tensor_tensor(lo[:, :, :], whole[:, :, :], hi[:, :, :].bitcast(F32), ALU.subtract
                                         ).then_inc(s_lo_pool, 1)

            def late():
                low_parts(EARLY_SPLITS, len(splits))

            def setup():
                low_parts(0, EARLY_SPLITS)
                pool.wait_ge(s_b_loaded, 16 * 3)

            steps(pool, step, setup, late)

        @block.scalar
        def _(act):
            sc = nc.scalar
            def store(g):
                dst = out[g * PAIR:(g + 1) * PAIR] if isinstance(g, int) else out[bass.ds(g * PAIR, PAIR)]
                act.dma_start(dst.rearrange("b p d -> p b d"), x_out[:, :, :]).then_inc(s_x_stored, 16)

            def normalise(l, n, src, used):
                act.wait_ge(s_terms[l], upto(n))
                for b in range(PAIR):
                    last = sc.activation(H[l][:, b, :], src[:, b, :], ACT.Relu,
                                         bias=nmr[l][:, b, 0:1], scale=rstd[l][:, b, 0:1])
                last.then_inc(s_h[l], 1)

            def high(l, n):
                act.wait_ge(s_turned[l], upto(n))
                sc.activation(hT_hi[l][:, :, :, :], quarters(TBANK[l]), ACT.Copy).then_inc(s_hi[l], 1)

            def hidden_relu(b, n):
                act.wait_ge(s_o1_made[b], upto(n))
                sc.activation(r3[:, b, :], o1[:, b, :], ACT.Relu).then_inc(s_r3_made[b], 1)

            def hidden_high(b, n):
                act.wait_ge(s_h1T_mm[b], upto(n))
                sc.activation(h1T_hi[:, b, :, :], bank[3 + b][:, :].rearrange("p (k n) -> p k n", k=K),
                              ACT.Copy).then_inc(s_h1T_hi[b], 1)

            def step(t, live):
                if live(1):
                    normalise(1, t, X[1], s_turned[1])
                if live(4):
                    act.wait_ge(s_G_out, upto(t - 3))
                    act.wait_ge(s_Gz_mm, upto(t - 4))
                    sc.activation(G_kept[:, :, :], G[:, :, 0:P], ACT.Copy).then_inc(s_G_kept, 1)
                if live(1):
                    high(1, t)
                if live(4):
                    hidden_relu(0, t - 3)
                if live(2):
                    normalise(2, t - 1, X[2], s_turned[2])
                if live(4):
                    hidden_relu(1, t - 3)
                if live(0):
                    act.wait_ge(s_tT_mm, upto(t + 1))
                    sc.activation(tT[:, :, :, :], quarters(0), ACT.Copy).then_inc(s_tT_out, 1)
                if live(1):
                    act.wait_ge(s_uT_mm, upto(t))
                    for m in range(C):
                        last = sc.activation(uT[:, m, :, :], quarters(5)[:, m, :, :], ACT.Identity,
                                             bias=ubias[:, m:m + 1])
                    last.then_inc(s_uT_out, 1)
                if live(2):
                    high(2, t - 1)
                if live(3):
                    act.wait_ge(s_binv_made, upto(t - 2))
                    for b in range(PAIR):
                        last = sc.activation(bHT[:, b, 0:P], HT[:, b, :], ACT.Copy, scale=binv[:, b:b + 1])
                    last.then_inc(s_bHT_made, 1)
                if live(1):
                    act.wait_ge(s_V1_mm, upto(t))
                    for b in range(PAIR):
                        last = sc.activation(v1[:, b, :], bank[VBANK[b]][:, 0:D], ACT.Copy)
                    last.then_inc(s_V1_out, 1)
                if live(5):
                    act.wait_ge(s_final[3], upto(t - 4))
                    store(t - 5)
                if live(1):
                    act.wait_ge(s_S1_mm, upto(t))
                    act.wait_ge(s_r1_out, upto(t))
                    for b in range(PAIR):
                        last = sc.activation(e1[:, b, :], small(1)[:, b, :], ACT.Exp, bias=r1[:, b:b + 1])
                    last.then_inc(s_e1_made, 1)
                if live(4):
                    hidden_high(0, t - 3)
                if live(2):
                    act.wait_ge(s_s2_made, upto(t - 1))
                    for b in range(PAIR):
                        last = sc.activation(th2[:, b, :], small(0)[:, b, :], ACT.Tanh,
                                             bias=s2[:, b:b + 1], scale=0.125)
                    last.then_inc(s_tanh_made, 1)
                if live(3):
                    act.wait_ge(s_G_mm, upto(t - 2))
                    sc.activation(G[:, :, :], gram, ACT.Copy).then_inc(s_G_out, 1)
                if live(4):
                    hidden_high(1, t - 3)
                if live(2):
                    act.wait_ge(s_lr_made, upto(t - 1))
                    sc.activation(e2[:, :, :], lr2[:, :, :], ACT.Exp, scale=8.0).then_inc(s_e2_made, 1)
                if live(2):
                    act.wait_ge(s_y_mm, upto(t - 1))
                    sc.activation(y2[:, :, :], halves(6), ACT.Copy).then_inc(s_y_out, 1)
                if live(0):
                    act.wait_ge(s_nmax_made, upto(t + 1))
                    sc.activation(erow[:, :], wrow[:, :], ACT.Exp, bias=nmax[:, :], accum_out=esum[:, :]
                                  ).then_inc(s_erow_made, 1)
                if live(3):
                    normalise(3, t - 2, X[3], s_agg_mm)
                if live(-1):
                    normalise(0, t + 2, x_in, s_turned[0])
                if live(2):
                    act.wait_ge(s_AT_mm, upto(t - 1))
                    sc.activation(a2T[:, :, :], bank[6][:, 256:512].rearrange("p (b n) -> p b n", b=PAIR), ACT.Copy
                                  ).then_inc(s_AT_out, 1)
                if live(1):
                    act.wait_ge(s_PT_mm, upto(t))
                    sc.activation(p1T[:, :, :], small(6), ACT.Copy).then_inc(s_PT_out, 1)
                if live(3):
                    act.wait_ge(s_agg_mm, upto(t - 2))
                    sc.activation(aggT_hi[:, :, :, :], quarters(1), ACT.Copy).then_inc(s_agg_hi, 1)
                if live(-1):
                    act.wait_ge(s_x_loaded, upto(t + 2, 16))
                    act.wait_ge(s_final[0], upto(t + 1))
                    sc.activation(X[0][:, :, :], x_in[:, :, :], ACT.Copy).then_inc(s_x0_copied, 1)
                if live(-1):
                    high(0, t + 2)
                if live(-1):
                    act.wait_ge(s_turned[0], upto(t + 2))
                    sc.activation(hT[0][:, :, :, :], quarters(6), ACT.Copy).then_inc(s_full[0], 1)

            def setup():
                act.wait_ge(s_cols_loaded, 16 * 5)
                act.wait_ge(s_ident_made, 1)
                for c in range(C):
                    sc.activation(a_rep[:, c, :], ones[:, :], ACT.Copy, scale=a_col[:, c:c + 1])
                    sc.activation(bq_rep[:, c, :], ones[:, :], ACT.Copy, scale=bq_col[:, c:c + 1])
                for k in range(K):
                    last = sc.activation(beta_rep[:, k, :], ones[:, :], ACT.Copy, scale=beta_col[:, k:k + 1])
                last.then_inc(s_reps_made, 1)
                high_parts(0, EARLY_SPLITS)

            def high_parts(first, end):
                for whole, (hi, lo), ready, n, _ in splits[first:end]:
                    act.wait_ge(ready, n)
                    sc.activation(hi[:, :, :], whole[:, :, :], ACT.Copy).then_inc(s_hi_done, 1)

            def late():
                high_parts(EARLY_SPLITS, len(splits))

            steps(act, step, setup, late)
            act.wait_ge(s_x_stored, 16 * NG)

        @block.vector
        def _(dve):
            v = nc.vector
            def stats_of(l, n, src):
                for b in range(PAIR):
                    last = v.bn_stats(stats[l][:, b, :], src[:, b, :])
                last.then_inc(s_stats[l], 1)

            def aggregate(l, n):
                dve.wait_ge(s_stats[l], upto(n))
                v.memset(dve_scratch[:, l:l + 1], 0.0)
                for b in range(PAIR):
                    last = v.bn_aggr(mv[l][:, b, :], stats[l][:, b, :])
                last.then_inc(s_mv[l], 1)

            def low(l, n):
                dve.wait_ge(s_hi[l], upto(n))
                v.tensor_tensor(hT_lo[l][:, :, :, :].rearrange("p c b n -> p (c b n)"), bank[TBANK[l]][:, :],
                                       hT_hi[l][:, :, :, :].bitcast(F32).rearrange("p c b n -> p (c b n)"),
                                ALU.subtract).then_inc(s_lo[l], 1)

            def hidden_low(b, n):
                dve.wait_ge(s_h1T_hi[b], upto(n))
                v.tensor_tensor(h1T_lo[:, b, :, :], bank[3 + b][:, :].rearrange("p (k n) -> p k n", k=K),
                                h1T_hi[:, b, :, :].bitcast(F32), ALU.subtract).then_inc(s_h1T_lo[b], 1)

            def hidden_out(b, n):
                dve.wait_ge(s_O1_mm[b], upto(n))
                dve.wait_ge(s_Dn_made, upto(n))
                v.scalar_tensor_tensor(o1[:, b, :], bank[3 + b][:, :], Dn[:, b:b + 1],
                                       b1_bc[:, :], ALU.mult, ALU.add).then_inc(s_o1_made[b], 1)

            def weighted_sum(dst, prod, acc, scale):
                for b in range(PAIR):
                    last = v.tensor_tensor_reduce(out=dst[:, b, :], in0=prod[0][:, b, :], in1=prod[1][:, b, :],
                                                  scale=scale, scalar=0.0, op0=ALU.mult, op1=ALU.add,
                                                  accum_out=acc[:, b:b + 1])
                return last

            def step(t, live):
                if live(4):
                    dve.wait_ge(s_dinv_made, upto(t - 3))
                    dve.wait_ge(s_final[3], upto(t - 4))
                    v.scalar_tensor_tensor(Dn[:, :], G[:, :, P], 0.0, dinv[:, :], ALU.is_gt, ALU.mult
                                           ).then_inc(s_Dn_made, 1)
                if live(2):
                    aggregate(2, t - 1)
                if live(4):
                    hidden_out(0, t - 3)
                if live(1):
                    low(1, t)
                if live(3):
                    dve.wait_ge(s_AdT_mm, upto(t - 2))
                    for b in range(PAIR):
                        v.tensor_scalar(HT[:, b, :], small(7)[:, b, :], 0.0, 0.0, ALU.not_equal, ALU.add,
                                        accum_out=cnt[:, b:b + 1])
                    v.tensor_copy(bHT[:, :, P], small(7)[:, :, 0]).then_inc(s_HT_made, 1)
                if live(4):
                    hidden_out(1, t - 3)
                if live(3):
                    dve.wait_ge(s_HT_made, upto(t - 2))
                    v.tensor_scalar(cnt1[:, :], cnt[:, :], 1.0, None, ALU.max).then_inc(s_cnt1_made, 1)
                if live(4):
                    for b in range(PAIR):
                        dve.wait_ge(s_r3_made[b], upto(t - 3))
                        last = v.bn_stats(stats[4][:, b, :], r3[:, b, :])
                    last.then_inc(s_stats[4], 1)
                if live(4):
                    aggregate(4, t - 3)
                if live(-1):
                    dve.wait_ge(s_x_loaded, upto(t + 2, 16))
                    stats_of(0, t + 2, x_in)
                if live(3):
                    dve.wait_ge(s_cnt1_made, upto(t - 2))
                    v.reciprocal(binv[:, :], cnt1[:, :]).then_inc(s_binv_made, 1)
                if live(2):
                    low(2, t - 1)
                if live(4):
                    dve.wait_ge(s_rstd[4], upto(t - 3))
                    for b in range(PAIR):
                        last = v.tensor_scalar(h1n[:, b, :], r3[:, b, :], mv[4][:, b, 0:1], rstd[4][:, b, 0:1],
                                               ALU.subtract, ALU.mult)
                    last.then_inc(s_h1n_made, 1)
                if live(1):
                    dve.wait_ge(s_V1_out, upto(t))
                    for b in range(PAIR):
                        last = v.tensor_scalar(r1[:, b:b + 1], bank[VBANK[b]][:, D:D + 1], rconst, None, ALU.add)
                    last.then_inc(s_r1_out, 1)
                if live(3):
                    dve.wait_ge(s_final[2], upto(t - 2))
                    stats_of(3, t - 2, X[3])
                if live(2):
                    dve.wait_ge(s_sb_mm, upto(t - 1))
                    for b in range(PAIR):
                        last = v.tensor_tensor_reduce(out=junk[:, b, :], in0=small(0)[:, b, :], in1=ident[:, :],
                                                      scale=0.125, scalar=0.0, op0=ALU.mult, op1=ALU.add,
                                                      accum_out=s2[:, b:b + 1])
                    last.then_inc(s_s2_made, 1)
                if live(3):
                    aggregate(3, t - 2)
                if live(4):
                    hidden_low(0, t - 3)
                if live(2):
                    dve.wait_ge(s_tanh_made, upto(t - 1))
                    v.scalar_tensor_tensor(lr2[:, :, :], th2[:, :, :], 0.1, th2[:, :, :], ALU.mult, ALU.max
                                           ).then_inc(s_lr_made, 1)
                if live(0):
                    dve.wait_ge(s_S0_mm, upto(t + 1))
                    dve.wait_ge(s_adm_made, upto(t + 1))
                    weighted_sum(junk0, (small(1), adm), w0, INV).then_inc(s_w0_made, 1)
                if live(4):
                    hidden_low(1, t - 3)
                if live(2):
                    dve.wait_ge(s_a2_loaded, upto(t - 1, 16))
                    v.tensor_reduce(asum2[:, :], AD[2][:, :, :], AX_X, ALU.add)
                if live(-1):
                    aggregate(0, t + 2)
                if live(3):
                    dve.wait_ge(s_G_out, upto(t - 2))
                    v.tensor_scalar(deg1[:, :], G[:, :, P], TINY, None, ALU.max).then_inc(s_deg1_made, 1)
                if live(0):
                    dve.wait_ge(s_wT_mm, upto(t + 1))
                    dve.wait_ge(s_mrow_loaded, upto(t + 1, 16))
                    v.tensor_tensor(wrow[:, :], bank[7][0:PAIR, 0:P], mask_rows[:, :], ALU.mult
                                    ).then_inc(s_wrow_made, 1)
                if live(0):
                    dve.wait_ge(s_wrow_made, upto(t + 1))
                    v.tensor_reduce(nmax[:, :], wrow[:, :], AX_X, ALU.max, negate=True).then_inc(s_nmax_made, 1)
                if live(1):
                    dve.wait_ge(s_e1_made, upto(t))
                    dve.wait_ge(s_a1_loaded, upto(t, 16))
                    weighted_sum(p1, (e1, AD[1]), sum1, 1.0).then_inc(s_p1_made, 1)
                if live(0):
                    dve.wait_ge(s_erow_made, upto(t + 1))
                    v.reciprocal(einv[:, :], esum[:, :]).then_inc(s_einv_made, 1)
                if live(0):
                    dve.wait_ge(s_einv_made, upto(t + 1))
                    v.tensor_scalar(prow[:, :], erow[:, :], einv[:, :], None, ALU.mult).then_inc(s_prow_made, 1)
                if live(2):
                    dve.wait_ge(s_e2_made, upto(t - 1))
                    dve.wait_ge(s_a2_loaded, upto(t - 1, 16))
                    weighted_sum(a2m, (e2, AD[2]), sum2, 1.0).then_inc(s_a2_made, 1)
                if live(4):
                    dve.wait_ge(s_z_mm, upto(t - 3))
                    v.tensor_tensor(z[:, :, :], halves(0), bw2[:, :].unsqueeze(1).broadcast_to([P, PAIR, D]),
                                    ALU.add).then_inc(s_z_out, 1)
                if live(3):
                    dve.wait_ge(s_deg1_made, upto(t - 2))
                    v.reciprocal(dinv[:, :], deg1[:, :]).then_inc(s_dinv_made, 1)
                if live(0):
                    dve.wait_ge(s_soft_mm, upto(t + 1))
                    v.tensor_copy(soft[:, :], bank[7][:, 0:PAIR]).then_inc(s_soft_out, 1)
                if live(2):
                    dve.wait_ge(s_a2_made, upto(t - 1))
                    v.reciprocal(inv2[:, :], sum2[:, :]).then_inc(s_inv2_made, 1)
                if live(0):
                    dve.wait_ge(s_soft_out, upto(t + 1))
                    dve.wait_ge(s_V0_mm, upto(t + 1))
                    dve.wait_ge(s_x0_copied, upto(t + 1))
                    dve.wait_ge(s_xv1_made, upto(t))
                    for b in range(PAIR):
                        last = v.scalar_tensor_tensor(X[1][:, b, :], halves(5)[:, b, :], soft[:, b:b + 1],
                                                      X[0][:, b, :], ALU.mult, ALU.add)
                    last.then_inc(s_final[0], 1)
                if live(2):
                    dve.wait_ge(s_inv2_made, upto(t - 1))
                    v.tensor_tensor(ratio2[:, :], inv2[:, :], asum2[:, :], ALU.mult).then_inc(s_ratio_made, 1)
                if live(0):
                    dve.wait_ge(s_final[0], upto(t + 1))
                    stats_of(1, t + 1, X[1])
                if live(1):
                    dve.wait_ge(s_p1_made, upto(t))
                    v.reciprocal(inv1[:, :], sum1[:, :]).then_inc(s_inv1_made, 1)
                if live(0):
                    aggregate(1, t + 1)
                if live(3):
                    dve.wait_ge(s_agg_hi, upto(t - 2))
                    v.tensor_tensor(aggT_lo[:, :, :, :].rearrange("p c b n -> p (c b n)"), bank[1][:, :],
                                    aggT_hi[:, :, :, :].bitcast(F32).rearrange("p c b n -> p (c b n)"), ALU.subtract
                                    ).then_inc(s_agg_lo, 1)
                if live(2):
                    dve.wait_ge(s_Ay_mm, upto(t - 1))
                    dve.wait_ge(s_ratio_made, upto(t - 1))
                    dve.wait_ge(s_final[1], upto(t - 1))
                    for b in range(PAIR):
                        last = v.scalar_tensor_tensor(X[3][:, b, :], halves(4)[:, b, :], ratio2[:, b:b + 1],
                                                      X[2][:, b, :], ALU.mult, ALU.add)
                    last.then_inc(s_final[2], 1)
                if live(1):
                    dve.wait_ge(s_inv1_made, upto(t))
                    dve.wait_ge(s_PV_mm, upto(t))
                    dve.wait_ge(s_xv1_made, upto(t))
                    dve.wait_ge(s_final[2], upto(t - 1))
                    for b in range(PAIR):
                        last = v.scalar_tensor_tensor(X[2][:, b, :], halves(2)[:, b, :], inv1[:, b:b + 1],
                                                      xv1[:, b, :], ALU.mult, ALU.add)
                    last.then_inc(s_final[1], 1)
                if live(4):
                    dve.wait_ge(s_Dn_made, upto(t - 3))
                    dve.wait_ge(s_Gz_mm, upto(t - 3))
                    dve.wait_ge(s_xb3_made, upto(t - 3))
                    dve.wait_ge(s_x_stored, upto(t - 4, 16))
                    for b in range(PAIR):
                        last = v.scalar_tensor_tensor(x_out[:, b, :], halves(0)[:, b, :], Dn[:, b:b + 1],
                                                      xb3[:, b, :], ALU.mult, ALU.add)
                    last.then_inc(s_final[3], 1)
                if live(1):
                    dve.wait_ge(s_final[1], upto(t))
                    stats_of(2, t, X[2])

            def low_part(i):
                whole, (hi, lo), _, _, _ = splits[i]
                dve.wait_ge(s_hi_done, i + 1)
                v.tensor_tensor(lo[:, :, :], whole[:, :, :], hi[:, :, :].bitcast(F32), ALU.subtract
                                ).then_inc(s_lo_vector, 1)

            def copies_out(first, end):
                for j in range(first, end):
                    dve.wait_ge(s_wturned, j + 1)
                    dst, kind = turn_jobs[j]
                    b = TURN_BANKS[j]
                    if kind == "gamma":
                        k0 = dst
                        v.tensor_copy(w32_t[:, k0:k0 + 2, :], halves(b))
                        for k in range(2):
                            last = v.tensor_scalar(w32_g[:, k0 + k, :], halves(b)[:, k, :],
                                                   gamma_col[:, k0 + k:k0 + k + 1], None, ALU.mult)
                        last.then_inc(s_turned_out, 1)
                    elif kind == "vecs":
                        v.tensor_copy(dst, bank[b][:, 0:5])
                        v.tensor_copy(wv1_t[:, :, D], bank[b][:, 2:4]).then_inc(s_turned_out, 1)
                    else:
                        v.tensor_copy(dst, bank[b][:, 0:kind]).then_inc(s_turned_out, 1)

            def setup():
                copies_out(0, 6)
                low_part(0)
                copies_out(6, 7)
                low_part(3)
                dve.wait_ge(s_cols_loaded, 16 * 5)
                copies_out(7, EARLY_TURNS)
                dve.wait_ge(s_b_loaded, 16 * 3)

            def late():
                copies_out(EARLY_TURNS, TURNS)
                low_part(5)
                low_part(6)

            steps(dve, step, setup, late)

        @block.tensor
        def _(pe):
            mm = nc.tensor.matmul

            def turn(dst, src):
                return nc.tensor.transpose(dst, src, ident[:, :])

            def product(dst, terms):
                for i, (a, b) in enumerate(terms):
                    last = mm(dst, a, b, start=(i == 0), stop=(i == len(terms) - 1))
                return last

            def split_product(dst, terms):
                return product(dst, [(x, y) for (ah, al), (bh, bl) in terms
                                     for x, y in ((ah, bl), (al, bh), (ah, bh))])

            def chunk(c):
                return slice(c * P, (c + 1) * P)

            def blocks(b, src, rows, cols):
                i = 0
                for c in cols:
                    for r in rows:
                        last = turn(bank[b][:, i * P:(i + 1) * P], src[:, r, chunk(c)])
                        i += 1
                return last

            def job_bank(j):
                return TURN_BANKS[j]

            def early():
                pe.wait_ge(s_ident_made, 1)
                pe.wait_ge(s_wqk0_loaded, 16)
                blocks(job_bank(0), rwqk0, range(C), range(0, C)).then_inc(s_wturned, 1)
                blocks(job_bank(1), rwqk0, range(C), range(C, 2 * C)).then_inc(s_wturned, 1)
                pe.wait_ge(s_wqk1_loaded, 16 * 2)
                for c in range(C):
                    last = product(halves(job_bank(2))[:, c, :],
                                   [(rwq1[:, a, chunk(c)], rwk1[:, a, :]) for a in range(C)])
                last.then_inc(s_wturned, 1)

            def setup():
                pe.wait_ge(s_turned_out, 2)
                for c in range(C):
                    last = product(halves(job_bank(3))[:, c, :],
                                   [(wq0_t[:, a, chunk(c)], wk0_t[:, a, :]) for a in range(C)])
                last.then_inc(s_wturned, 1)
                pe.wait_ge(s_w3_loaded, 16 * 2)
                blocks(job_bank(4), rw31, range(K), range(0, 1)).then_inc(s_wturned, 1)
                blocks(job_bank(5), rw31, range(K), range(1, 2)).then_inc(s_wturned, 1)
                pe.wait_ge(s_reps_made, 1)
                v = bank[job_bank(6)]
                for c in range(C):
                    product(v[:, c:c + 1], [(rwk1[:, a, chunk(c)], bq_col[:, a:a + 1]) for a in range(C)])
                    product(v[:, 2 + c:3 + c], [(rwq1[:, a, chunk(c)], bk_col[:, a:a + 1]) for a in range(C)])
                product(v[:, 4:5], [(bq_rep[:, a, :], bk_col[:, a:a + 1]) for a in range(C)]).then_inc(s_wturned, 1)
                pe.wait_ge(s_w2_loaded, 16)
                pe.wait_ge(s_turned_out, 3)
                blocks(job_bank(7), rw2, range(C), range(C)).then_inc(s_wturned, 1)
                pe.wait_ge(s_wv1_loaded, 16)
                pe.wait_ge(s_turned_out, 4)
                blocks(job_bank(8), rwv1, range(C), range(C)).then_inc(s_wturned, 1)
                pe.wait_ge(s_turned_out, 5)
                blocks(job_bank(9), rw32, range(C), range(0, 2)).then_inc(s_wturned, 1)
                pe.wait_ge(s_hi[0], 1)
                pe.wait_ge(s_full[0], 1)
                blocks(job_bank(10), rw32, range(C), range(2, 4)).then_inc(s_wturned, 1)
                pe.wait_ge(s_turned_out, 7)
                pe.wait_ge(s_lo_pool, 1)

            def late():
                pe.wait_ge(s_turned_out, EARLY_TURNS)
                for c in range(C):
                    last = product(small(job_bank(11))[:, c, :],
                                   [(w2_t[:, a, chunk(c)], a_rep[:, a, :]) for a in range(C)])
                last.then_inc(s_wturned, 1)
                product(bank[job_bank(12)][:, 0:D],
                        [(beta_rep[:, k, :], w32_t[:, k, :]) for k in range(K)]).then_inc(s_wturned, 1)
                pe.wait_ge(s_lo_vector, LO_VECTOR)
                pe.wait_ge(s_lo_pool, LO_POOL)

            def turn_pair(b, src):
                for c in range(C):
                    for g in range(PAIR):
                        last = turn(quarters(b)[:, c, g, :], src[:, g, chunk(c)])
                return last

            def mix(b, w, l):
                for m in range(C):
                    last = split_product(bank[b][:, m * 256:(m + 1) * 256],
                                         [((w[0][:, c, chunk(m)], w[1][:, c, chunk(m)]),
                                           (hT_hi[l][:, c, :, :], hT_lo[l][:, c, :, :])) for c in range(C)])
                return last

            def project(b, w, l):
                for g in range(PAIR):
                    last = split_product(halves(b)[:, g, :],
                                         [((hT_hi[l][:, c, g, :], hT_lo[l][:, c, g, :]),
                                           (w[0][:, c, :], w[1][:, c, :])) for c in range(C)])
                return last

            def hidden_product(g):
                return split_product(halves(0)[:, g, :],
                                     [((h1T_hi[:, g, k, :], h1T_lo[:, g, k, :]),
                                       (w32_p[0][:, k, :], w32_p[1][:, k, :])) for k in range(K)])

            def turn_hidden(g):
                for k in range(K):
                    last = turn(bank[3 + g][:, k * P:(k + 1) * P], h1n[:, g, chunk(k)])
                return last

            def first_weights(g):
                for j in range(DH // 256):
                    cols = slice(j * 256, (j + 1) * 256)
                    last = split_product(bank[3 + g][:, cols],
                                         [((aggT_hi[:, c, g, :], aggT_lo[:, c, g, :]),
                                           (w31_p[0][:, c, cols], w31_p[1][:, c, cols])) for c in range(C)])
                return last

            def scores(b, left, l):
                for g in range(PAIR):
                    last = product(small(b)[:, g, :], [(left[:, c, g, :], hT[l][:, c, g, :]) for c in range(C)])
                return last

            def step(t, live):
                if live(5):
                    pe.wait_ge(s_G_kept, upto(t - 4))
                    pe.wait_ge(s_z_out, upto(t - 4))
                    for g in range(PAIR):
                        last = product(halves(0)[:, g, :], [(G_kept[:, g, :], z[:, g, :])])
                    last.then_inc(s_Gz_mm, 1)
                if live(4):
                    pe.wait_ge(s_agg_lo, upto(t - 3))
                    first_weights(0).then_inc(s_O1_mm[0], 1)
                if live(3):
                    pe.wait_ge(s_a3_loaded, upto(t - 2, 16))
                    pe.wait_ge(s_soft_out, upto(t))
                    for b in range(PAIR):
                        last = turn(small(7)[:, b, :], AD[3][:, b, :])
                    last.then_inc(s_AdT_mm, 1)
                if live(1):
                    pe.wait_ge(s_h[1], upto(t))
                    turn_pair(1, H[1]).then_inc(s_turned[1], 1)
                if live(4):
                    pe.wait_ge(s_agg_lo, upto(t - 3))
                    pe.wait_ge(s_final[2], upto(t - 2))
                    first_weights(1).then_inc(s_O1_mm[1], 1)
                if live(0):
                    pe.wait_ge(s_lo[0], upto(t + 1))
                    pe.wait_ge(s_final[3], upto(t - 4))
                    mix(0, m0_p, 0).then_inc(s_tT_mm, 1)
                if live(1):
                    pe.wait_ge(s_lo[1], upto(t))
                    mix(5, m1_p, 1).then_inc(s_uT_mm, 1)
                if live(2):
                    pe.wait_ge(s_h[2], upto(t - 1))
                    turn_pair(3, H[2]).then_inc(s_turned[2], 1)
                if live(1):
                    pe.wait_ge(s_lo[1], upto(t))
                    pe.wait_ge(s_HT_made, upto(t - 2))
                    for g in range(PAIR):
                        last = split_product(bank[VBANK[g]][:, 0:DV],
                                             [((hT_hi[1][:, c, g, :], hT_lo[1][:, c, g, :]),
                                               (wv1_p[0][:, c, :], wv1_p[1][:, c, :])) for c in range(C)])
                    last.then_inc(s_V1_mm, 1)
                if live(1):
                    pe.wait_ge(s_full[1], upto(t))
                    pe.wait_ge(s_uT_out, upto(t))
                    scores(1, uT, 1).then_inc(s_S1_mm, 1)
                if live(2):
                    pe.wait_ge(s_lo[2], upto(t - 1))
                    split_product(bank[0][:, 0:256],
                                  [((wa_p[0][:, c, :], wa_p[1][:, c, :]),
                                    (hT_hi[2][:, c, :, :], hT_lo[2][:, c, :, :])) for c in range(C)]
                                  ).then_inc(s_sb_mm, 1)
                if live(3):
                    pe.wait_ge(s_bHT_made, upto(t - 2))
                    for g in range(PAIR):
                        last = product(gram[:, g, :], [(HT[:, g, :], bHT[:, g, :])])
                    last.then_inc(s_G_mm, 1)
                if live(4):
                    pe.wait_ge(s_h1n_made, upto(t - 3))
                    turn_hidden(0).then_inc(s_h1T_mm[0], 1)
                if live(4):
                    pe.wait_ge(s_h1n_made, upto(t - 3))
                    turn_hidden(1).then_inc(s_h1T_mm[1], 1)
                if live(0):
                    pe.wait_ge(s_tT_out, upto(t + 1))
                    pe.wait_ge(s_e1_made, upto(t))
                    scores(1, tT, 0).then_inc(s_S0_mm, 1)
                if live(2):
                    pe.wait_ge(s_lo[2], upto(t - 1))
                    project(6, w2_p, 2).then_inc(s_y_mm, 1)
                if live(0):
                    pe.wait_ge(s_w0_made, upto(t + 1))
                    turn(bank[7][0:PAIR, 0:P], w0[:, :]).then_inc(s_wT_mm, 1)
                if live(4):
                    pe.wait_ge(s_h1T_lo[0], upto(t - 3))
                    pe.wait_ge(s_tanh_made, upto(t - 1))
                    hidden_product(0)
                if live(4):
                    pe.wait_ge(s_h1T_lo[1], upto(t - 3))
                    hidden_product(1).then_inc(s_z_mm, 1)
                if live(0):
                    pe.wait_ge(s_lo[0], upto(t + 1))
                    pe.wait_ge(s_G_out, upto(t - 2))
                    project(5, wv0_p, 0).then_inc(s_V0_mm, 1)
                if live(0):
                    pe.wait_ge(s_prow_made, upto(t + 1))
                    product(bank[7][:, 0:PAIR], [(prow[:, :], ident[0:PAIR, 0:PAIR])]).then_inc(s_soft_mm, 1)
                if live(1):
                    pe.wait_ge(s_p1_made, upto(t))
                    pe.wait_ge(s_y_out, upto(t - 1))
                    for g in range(PAIR):
                        last = turn(small(6)[:, g, :], p1[:, g, :])
                    last.then_inc(s_PT_mm, 1)
                if live(2):
                    pe.wait_ge(s_a2_made, upto(t - 1))
                    pe.wait_ge(s_y_out, upto(t - 1))
                    for g in range(PAIR):
                        last = turn(bank[6][:, (2 + g) * P:(3 + g) * P], a2m[:, g, :])
                    last.then_inc(s_AT_mm, 1)
                if live(3):
                    pe.wait_ge(s_G_out, upto(t - 2))
                    pe.wait_ge(s_h[3], upto(t - 2))
                    for g in range(PAIR):
                        for c in range(C):
                            last = product(quarters(1)[:, c, g, :], [(H[3][:, g, chunk(c)], G[:, g, 0:P])])
                    last.then_inc(s_agg_mm, 1)
                if live(2):
                    pe.wait_ge(s_AT_out, upto(t - 1))
                    for g in range(PAIR):
                        last = product(halves(4)[:, g, :], [(a2T[:, g, :], y2[:, g, :])])
                    last.then_inc(s_Ay_mm, 1)
                if live(-1):
                    pe.wait_ge(s_h[0], upto(t + 2))
                    pe.wait_ge(s_PT_out, upto(t))
                    turn_pair(6, H[0]).then_inc(s_turned[0], 1)
                if live(1):
                    pe.wait_ge(s_PT_out, upto(t))
                    pe.wait_ge(s_V1_out, upto(t))
                    for g in range(PAIR):
                        last = product(halves(2)[:, g, :], [(p1T[:, g, :], v1[:, g, :])])
                    last.then_inc(s_PV_mm, 1)

            steps(pe, step, setup, late, early)


_INS = ["x", "adj", "nodemask", "L0_gnn_Wqk", "L0_gnn_Wv", "L1_gnn_Wq_w", "L1_gnn_Wq_b", "L1_gnn_Wk_w",
        "L1_gnn_Wk_b", "L1_gnn_Wv_w", "L1_gnn_Wv_b", "L2_gnn_w", "L2_gnn_a", "L3_gnn_W1", "L3_gnn_b1",
        "L3_gnn_gamma", "L3_gnn_beta", "L3_gnn_W2", "L3_gnn_b2"]


def kernel(**inputs):
    import numpy as np
    import concourse.bacc as bacc
    from concourse.bass_utils import run_bass_kernel_spmd as run

    nc = bacc.Bacc("TRN2", target_bir_lowering=False, num_devices=1)
    arrays, args = {}, []
    for name in _INS:
        a = np.ascontiguousarray(inputs[name])
        arrays[f"in_{name}_dram"] = a
        args.append(nc.dram_tensor(f"in_{name}_dram", a.shape, mybir.dt.from_np(a.dtype), kind="ExternalInput").ap())
    out = nc.dram_tensor("out_dram", arrays["in_x_dram"].shape, F32, kind="ExternalOutput").ap()
    build(nc, *args, out)
    return run(nc, [arrays], core_ids=[0]).results[0]["out_dram"]
```
